# Optimizing a Trainium2 kernel written in Bass

```python
import numpy as np
import jax
import jax.numpy as jnp

def _softmax(x, axis=-1):
    return jax.nn.softmax(x, axis=axis)

def _gelu(x):
    return jax.nn.gelu(x, approximate=True)

def _silu(x):
    return jax.nn.silu(x)

def _sigmoid(x):
    return jax.nn.sigmoid(x)

def _layernorm(x, axis=-1, eps=1e-05):
    m = jnp.mean(x, axis=axis, keepdims=True)
    v = jnp.var(x, axis=axis, keepdims=True)
    return (x - m) / jnp.sqrt(v + eps)

def _scatter_add(tgt, idx, src, axis=0):
    return tgt.at[idx].add(src)

def _segment_sum(src, seg, n):
    return jax.ops.segment_sum(src, seg, n)
kernel_name = 'mk_macaron_d1_jaxref_r8_edbf32'

def setup_inputs(seed: int=0):
    np.random.seed(seed)
    _w = jnp.asarray

    def _L0_attn_setup():
        import jax, jax.numpy as jnp
        import numpy as np
        import math
        HIDDEN = 256
        NUM_HEADS = 16
        HEAD_SIZE = HIDDEN // NUM_HEADS
        BATCH = 2
        SEQ = 256
        key = jax.random.key(seed)
        k_x, k_wq, k_bq, k_wo, k_bo = jax.random.split(key, 5)
        scale_in = 1.0 / math.sqrt(HIDDEN)
        return {'x': jax.random.normal(k_x, (BATCH, SEQ, HIDDEN), dtype=jnp.float32), 'Wqkv': jax.random.normal(k_wq, (HIDDEN, 3 * HIDDEN), dtype=jnp.float32) * scale_in, 'bqkv': jax.random.normal(k_bq, (3 * HIDDEN,), dtype=jnp.float32) * 0.01, 'Wo': jax.random.normal(k_wo, (HIDDEN, HIDDEN), dtype=jnp.float32) * scale_in, 'bo': jax.random.normal(k_bo, (HIDDEN,), dtype=jnp.float32) * 0.01}
    _L0_attn_in = _L0_attn_setup()

    def _L0_ffn_setup():
        import jax, jax.numpy as jnp
        import numpy as np
        B, S, D, H = (4, 256, 256, 1024)

        def fwht(x):
            orig_shape = x.shape
            n = orig_shape[-1]
            x = x.reshape(-1, n)
            h = 1
            while h < n:
                xb = x.reshape(-1, n // (2 * h), 2, h)
                a = xb[:, :, 0, :]
                b = xb[:, :, 1, :]
                x = jnp.stack([a + b, a - b], axis=2).reshape(-1, n)
                h *= 2
            scale = jnp.asarray(1.0 / np.sqrt(n), dtype=x.dtype)
            return (x * scale).reshape(orig_shape)
        key = jax.random.key(seed)
        kx, k1, k2, k3 = jax.random.split(key, 4)
        x = jax.random.normal(kx, (B, S, D), dtype=jnp.float32)
        W1 = jax.random.normal(k1, (H, D), dtype=jnp.float32) * (1.0 / np.sqrt(D))
        W2 = jax.random.normal(k2, (D, H), dtype=jnp.float32) * (1.0 / np.sqrt(H))
        W3 = jax.random.normal(k3, (H, D), dtype=jnp.float32) * (1.0 / np.sqrt(D))
        return {'x': x, 'W1': W1, 'W2': W2, 'W3': W3}
    _L0_ffn_in = _L0_ffn_setup()
    _d = {'L0_attn_x': _L0_attn_in['x'], 'L0_attn_Wqkv': _L0_attn_in['Wqkv'], 'L0_attn_bqkv': _L0_attn_in['bqkv'], 'L0_attn_Wo': _L0_attn_in['Wo'], 'L0_attn_bo': _L0_attn_in['bo'], 'L0_ffn_W1': _L0_ffn_in['W1'], 'L0_ffn_W2': _L0_ffn_in['W2'], 'L0_ffn_W3': _L0_ffn_in['W3']}
    _x0 = _d['L0_attn_x']
    _d['L0_attn_x'] = jax.random.normal(jax.random.fold_in(jax.random.key(seed), 1), (2, 1024, 256), dtype=_x0.dtype)
    del _x0
    return _d

def reference(L0_attn_x, L0_attn_Wqkv, L0_attn_bqkv, L0_attn_Wo, L0_attn_bo, L0_ffn_W1, L0_ffn_W2, L0_ffn_W3):

    def _L0_attn_ref(x, Wqkv, bqkv, Wo, bo):
        import jax, jax.numpy as jnp
        import numpy as np
        import math
        HIDDEN = 256
        NUM_HEADS = 16
        HEAD_SIZE = HIDDEN // NUM_HEADS
        BATCH = 2
        SEQ = 256
        b, s, _ = x.shape
        kqv = x @ Wqkv + bqkv
        kqv = kqv.reshape(b, s, 3, NUM_HEADS, HEAD_SIZE)
        q = kqv[:, :, 0]
        k = kqv[:, :, 1]
        v = kqv[:, :, 2]
        scores = jnp.einsum('bsnh,btnh->bnst', k, q) / math.sqrt(HEAD_SIZE)
        ones = jnp.ones_like(scores)
        scores = jnp.triu(scores) + -10000.0 * jnp.tril(ones, k=-1)
        attn = jax.nn.softmax(scores, axis=2)
        out = jnp.einsum('bnkq,bknh->bqnh', attn, v)
        out = out.reshape(b, s, NUM_HEADS * HEAD_SIZE)
        return out @ Wo + bo

    def _L0_ffn_ref(x, W1, W2, W3):
        import jax, jax.numpy as jnp
        import numpy as np
        B, S, D, H = (4, 256, 256, 1024)

        def fwht(x):
            orig_shape = x.shape
            n = orig_shape[-1]
            x = x.reshape(-1, n)
            h = 1
            while h < n:
                xb = x.reshape(-1, n // (2 * h), 2, h)
                a = xb[:, :, 0, :]
                b = xb[:, :, 1, :]
                x = jnp.stack([a + b, a - b], axis=2).reshape(-1, n)
                h *= 2
            scale = jnp.asarray(1.0 / np.sqrt(n), dtype=x.dtype)
            return (x * scale).reshape(orig_shape)
        up_gate = jnp.einsum('bsd,hd->bsh', x, W1)
        up_lin = jnp.einsum('bsd,hd->bsh', x, W3)
        hidden = jax.nn.silu(up_gate) * up_lin
        hidden = fwht(hidden)
        out = jnp.einsum('bsh,dh->bsd', hidden, W2)
        return out
    x = L0_attn_x
    x = x + 0.5 * _L0_ffn_ref(_layernorm(x, axis=-1), L0_ffn_W1, L0_ffn_W2, L0_ffn_W3)
    x = x + _L0_attn_ref(_layernorm(x, axis=-1), L0_attn_Wqkv, L0_attn_bqkv, L0_attn_Wo, L0_attn_bo)
    x = x + 0.5 * _L0_ffn_ref(_layernorm(x, axis=-1), L0_ffn_W1, L0_ffn_W2, L0_ffn_W3)
    return x

_drawn_inputs = setup_inputs


def setup_inputs(seed=0):
    import zlib

    import numpy as np

    out = dict(_drawn_inputs(seed))
    spreads = {}
    factors = {'L0_attn_bqkv': 5.302, 'L0_attn_bo': 6.434}
    for name, (base, spread) in spreads.items():
        noise = np.random.default_rng([zlib.crc32(name.encode()), seed]).standard_normal(out[name].shape)
        drawn = base * np.exp(spread * noise) if base else spread * noise
        out[name] = jnp.asarray(drawn.astype(out[name].dtype))
    for name, factor in factors.items():
        out[name] = (out[name] * factor).astype(out[name].dtype)
    return out
```

```python
from contextlib import ExitStack

import numpy as np

import concourse.bass as bass
from concourse import mybir

F32 = mybir.dt.float32
F32R = mybir.dt.float32r
BF16 = mybir.dt.bfloat16
ACT = mybir.ActivationFunctionType
ALU = mybir.AluOpType
AX = mybir.AxisListType

P = 128
BATCH, SEQ, D = 2, 1024, 256
HIDDEN = 1024
HEADS, HD = 16, 16
TOKENS = BATCH * SEQ
CH = 512
NC = TOKENS // CH
TPC = CH // P
ND = D // P
NH = HIDDEN // P
GH = 4
GROUPS = HEADS // GH
UNITS = BATCH * GROUPS
KT = SEQ // P
VW = 32
PARTS = 3
Q_PART = (0, 0, 0, 1, 1, 2)
K_PART = (0, 1, 2, 0, 1, 0)
STACK_LOADS = len(Q_PART) + len(K_PART)
QBUF = 4
SROWS = 6 * HD
MROWS = SROWS + PARTS
EPS = 1e-5
SCALE = 1.0 / float(np.sqrt(HD))
MASKED = -10000.0
NEG_BIG = -1e30

STEPS = [(c, j, max(0, j * P - c * CH)) for c in range(2) for j in range(KT) if j * P < (c + 1) * CH]
NSTEP = len(STEPS)
STEPS_C0 = sum(1 for s in STEPS if s[0] == 0)
AHEAD = 3
DIAG = [s for s, (c, j, q0) in enumerate(STEPS) if j * P >= c * CH]

RED_A = [("red", i, h, 0) for i in range(KT // 2) for h in range(GH)]
RED_B = [("red", i, h, piece) for i in range(KT // 2, KT) for piece in range(2) for h in range(GH)]
NA, NB = len(RED_A), len(RED_B)
RING = 3


W2_SCALE = 0.5 / float(np.sqrt(HIDDEN))


def loop_wait(eng, sem, value):
    eng.wait_ge(sem, value)
    if not isinstance(value, int):
        eng.nop(nofuse=True)


def red_width(i, piece):
    return min(CH, (i + 1) * P - piece * CH)


def body_plan():
    reds = [(it, red_width(it[1], it[3]) + 120) for it in RED_A + RED_B]
    total = sum(w for _, w in reds)
    slots = [[] for _ in range(NSTEP)]
    spread = NSTEP - 1.0
    done = 0
    for n, (it, w) in enumerate(reds):
        at = min(NSTEP - 2, int(done * spread / total))
        slots[at].append(it)
        if n == NA + 3:
            slots[at].append(("mt", 0, 0, 0))
        done += w
    slots[STEPS_C0 - AHEAD + 2].append(("ot", 0, 0, 0))
    slots[NSTEP - AHEAD + 2] += [("ot", 1, 0, 0), ("mt", 1, 0, 0)]
    return slots


BODY = body_plan()
BODY_ITEMS = [it for s in BODY for it in s]
FIRST_ITEMS = RED_A + RED_B[:12] + [("mt", 0, 0, 0)] + RED_B[12:] + [("mt", 1, 0, 0)]
SUFFIX_FROM = 9
FIRST_GAP = 6
FIRST_SCORES = len(FIRST_ITEMS) - 1 - 2 * FIRST_GAP
LAST_ITEMS = [("ot", 0, 0, 0), ("ot", 1, 0, 0)]
NBODY, NFIRST = len(BODY_ITEMS), len(FIRST_ITEMS)
RING_TOTAL = NFIRST + (UNITS - 1) * NBODY + len(LAST_ITEMS)


def ring_count(unit, item):
    items = LAST_ITEMS if isinstance(unit, int) and unit == UNITS - 1 else BODY_ITEMS
    return unit * NBODY + (NFIRST + items.index(item) + 1)


def macaron(nc, x_d, w1t_d, w3t_d, w2t_d, wqkv_d, wo_d, bqk_d, bv_d, bo_d, had_d, ident_d, tri_d,
            after_d, count_d, floor_d, out_d):
    ctx = ExitStack()
    with ctx:
        def sb(name, shape, dt):
            return ctx.enter_context(nc.sbuf_tensor(name, shape, dt))

        def sem(name):
            return ctx.enter_context(nc.semaphore(name))

        x = sb("x", [P, NC * TPC, D], F32)
        w1 = sb("w1", [P, 2, ND, HIDDEN], F32R)
        w3 = sb("w3", [P, 2, ND, HIDDEN], F32R)
        w2 = sb("w2", [P, 2, NH, D], F32R)
        wo = sb("wo", [P, 2, ND, D], F32R)
        v_all = sb("v_all", [P, KT, UNITS, GH * HD], F32)

        def take_turns(*groups):
            made = []
            for g in groups[1:]:
                with ExitStack() as s:
                    made.append([s.enter_context(nc.sbuf_tensor(n, sh, t)) for n, sh, t in g])
            return [[sb(n, sh, t) for n, sh, t in groups[0]]] + made

        (xt,), (probs,) = take_turns([("xt", [P, NC, 2, ND, CH], F32R)],
                                     [("probs", [P, RING, GH, CH], F32)])
        (qs, ks), (w1_raw, w3_raw, w2_raw, wqkv_raw, wo_raw) = take_turns(
            [("qs", [MROWS, 2, 2, GH, CH], BF16), ("ks", [MROWS, 2, 2, GH, CH], BF16)],
            [("w1_raw", [P, ND, HIDDEN], F32), ("w3_raw", [P, ND, HIDDEN], F32), ("w2_raw", [P, NH, D], F32),
             ("wqkv_raw", [P, ND, 3 * D], F32), ("wo_raw", [P, ND, D], F32)])
        (o_tok,), (wqkv, qf) = take_turns([("o_tok", [P, KT, UNITS, GH * HD], F32)],
                                          [("wqkv", [P, 2, ND, 3 * D], F32R), ("qf", [P, 2, CH], F32)])
        (u, uh, ul), (vg, o_raw, num) = take_turns(
            [("u", [P, 2, CH], F32), ("uh", [P, 2, CH], F32R), ("ul", [P, 2, CH], F32R)],
            [("vg", [P, 2, KT, GH, VW], F32), ("o_raw", [P, CH], F32), ("num", [P, TPC, GH, HD], F32)])
        (suffix,), (r1, stage) = take_turns(
            [("suffix", [P, KT, UNITS, GH * HD], F32)],
            [("r1", [P, 2, CH], F32), ("stage", [P, QBUF, PARTS, CH], BF16)])
        xn = sb("xn", [P, TPC, D], F32)
        had = sb("had", [P, P], F32)
        ident = sb("ident", [P, P], F32)
        after = sb("after", [P, P], F32)
        ones = sb("ones", [P, P], F32)
        ident_b = sb("ident_b", [P, P], BF16)
        tri_f = sb("tri_f", [P, P], F32)
        tri_b = sb("tri_b", [P, P], BF16)
        bqk = sb("bqk", [P, 4], F32)
        bv = sb("bv", [P, D], F32)
        bo = sb("bo", [P, D], F32)
        count = sb("count", [P, KT], F32)
        neg_floor = sb("neg_floor", [P, GH, KT // 2], F32)
        bn = sb("bn", [P, TPC, 6], F32)
        mv = sb("mv", [P, TPC, 2], F32)
        ve = sb("ve", [P, TPC], F32)
        rstd = sb("rstd", [P, TPC], F32)
        neg_half = sb("neg_half", [P, TPC], F32)
        mp = sb("mp", [P, NA + NB], F32)
        mb = sb("mb", [P, GH, KT // 2], F32)
        mneg = sb("mneg", [P, 2, GH, KT], F32)
        mres = sb("mres", [P, 2, GH, KT // 2], F32)
        mpart = sb("mpart", [P, 2, PARTS, GH, KT // 2], BF16)
        MT = GH * KT // 2
        mt = sb("mt", [PARTS * MT, 2, P], BF16)
        ea = sb("ea", [P, GH, KT], F32)
        et = sb("et", [P, 2, GH, KT], F32)
        ecnt = sb("ecnt", [P, 2, GH, KT], F32)
        em = sb("em", [P, 2, KT, GH, HD], F32)
        dsum = sb("dsum", [P, TPC, GH], F32)
        rcp = sb("rcp", [P, TPC, GH], F32)

        banks = [ctx.enter_context(nc.psum_tensor(f"bank{i}", [P, CH], F32)) for i in range(4)]
        pair = [ctx.enter_context(nc.psum_tensor(f"pair{i}", [P, 2, CH], F32)) for i in range(2)]
        ps_gate, ps_lin = banks[0:2], banks[2:4]
        ps_down, ps_t = pair
        ps_ring, ps_o, ps_s = banks[0:3], banks[3], pair

        parts_d = nc.dram_tensor("parts", (2, UNITS, 2, GH * HD, PARTS, CH), BF16, kind="Internal").ap()

        ld_x = [sem(f"ld_x{c}") for c in range(NC)]
        ld_w1, ld_w3, ld_w2 = sem("ld_w1"), sem("ld_w3"), sem("ld_w2")
        ld_wqkv, ld_wo, ld_const = sem("ld_wqkv"), sem("ld_wo"), sem("ld_const")
        const_cut, pool_const, stack_ones, vg_ones = sem("const_cut"), sem("pool_const"), sem("stack_ones"), sem("vg_ones")
        bn_done, mv_done, ve_done = sem("bn_done"), sem("mv_done"), sem("ve_done")
        rstd_done, xn_done = sem("rstd_done"), sem("xn_done")
        xt_ps, xt_hi, xt_lo = sem("xt_ps"), sem("xt_hi"), sem("xt_lo")
        w13_hi, w13_lo, fly_sum, fly_diff = sem("w13_hi"), sem("w13_lo"), sem("fly_sum"), sem("fly_diff")
        had_ps, w2_hi, w2_lo = sem("had_ps"), sem("w2_hi"), sem("w2_lo")
        wsplit_hi, wsplit_lo = sem("wsplit_hi"), sem("wsplit_lo")
        gate_done, lin_done, silu_done = sem("gate_done"), sem("lin_done"), sem("silu_done")
        u_done, uh_done, ul_done = sem("u_done"), sem("uh_done"), sem("ul_done")
        down_used, down_done, res_added = sem("down_used"), sem("down_done"), sem("res_added")
        qk_ps, qf_done, qh_done, r1_done = sem("qk_ps"), sem("qf_done"), sem("qh_done"), sem("r1_done")
        qm_done, ql_done, v_ps, v_done = sem("qm_done"), sem("ql_done"), sem("v_ps"), sem("v_done")
        part_out = [sem(f"part_out{i}") for i in range(QBUF)]
        stack_in = [sem(f"stack_in{i}") for i in range(2)]
        mrow_in = [sem(f"mrow_in{i}") for i in range(2)]
        wsum_done, suf_ps, suf_done = sem("wsum_done"), sem("suf_ps"), sem("suf_done")
        vg_done, bo_added = sem("vg_done"), sem("bo_added")
        ring_full, ring_free = sem("ring_full"), sem("ring_free")
        mb_done, mneg_done, cut_step, mp_cut = sem("mb_done"), sem("mneg_done"), sem("cut_step"), sem("mp_cut")
        ea_step, ea_done, et_done, em_done = sem("ea_step"), sem("ea_done"), sem("et_done"), sem("em_done")
        s_ps, p_done, p_masked, pv_done = sem("s_ps"), sem("p_done"), sem("p_masked"), sem("pv_done")
        o_copied, dsum_done, rcp_done, num_done, o_done = (sem("o_copied"), sem("dsum_done"), sem("rcp_done"),
                                                           sem("num_done"), sem("o_done"))
        out_sent = sem("out_sent")

        FILLS = ([("IN", c) for c in range(NC)] + [("FF", c) for c in range(NC)]
                 + [("AT", 0), ("AT", 1), ("AT", 2), ("OUT", 0), ("AT", 3), ("OUT", 1), ("OUT", 2), ("OUT", 3)])

        def fill_no(kind, c):
            return FILLS.index((kind, c)) if isinstance(c, int) else {"IN": 0, "FF": NC}[kind] + c

        def norm_no(kind, c):
            return {"IN": 0, "FF": NC, "OUT": 2 * NC}[kind] + c

        RES = {"FF": 0, "OUT": NC, "FF2": 2 * NC}
        WSPLIT = 4
        WP = HIDDEN // WSPLIT

        def chunk_of(t, c):
            return t[:, bass.ds(c * TPC, TPC), :]

        LAST_FILL = 4
        CUTS = (4, 3)

        def fly_views(stage_no):
            fly = v_all[:, 0:NH // 2].rearrange("p j u n -> p (j u n)").rearrange("p (k n) -> p k n", n=D)
            places = (w2_raw[:], fly) if stage_no % 2 == 0 else (fly, w2_raw[:])
            src, dst = [t.rearrange("p (a two b) n -> p two a (b n)", two=2, b=1 << stage_no) for t in places]
            return src[:, 0], src[:, 1], dst[:, 0], dst[:, 1]

        def sent(projections, buf):
            return 16 * len(range(buf, projections, QBUF))

        def fly_out(i):
            return v_all[:, i].rearrange("p u n -> p (u n)")

        def w_sum(i):
            return xn[:, 2 * (i % 2):2 * (i % 2) + 2, :].rearrange("p a n -> p (a n)").rearrange("p (u n) -> p u n", u=UNITS)

        block = ctx.enter_context(nc.Block())

        @block.sync
        def _(sp):
            x_t = x_d.rearrange("(t p) n -> p t n", p=P)
            sp.dma_start(x[:, 0:TPC, :], x_t[:, 0:TPC, :]).then_inc(ld_x[0], 16)
            sp.dma_start(w1_raw[:], w1t_d.rearrange("(c p) n -> p c n", p=P)).then_inc(ld_w1, 16)
            for t, d_ in ((ident, ident_d), (had, had_d), (bqk, bqk_d), (neg_floor, floor_d), (tri_f, tri_d),
                          (after, after_d), (count, count_d)):
                sp.dma_start(t[:], d_).then_inc(ld_const, 16)
            sp.dma_start(w2_raw[:], w2t_d.rearrange("(c p) n -> p c n", p=P)).then_inc(ld_w2, 16)
            for c in range(1, NC):
                sp.dma_start(chunk_of(x, c), chunk_of(x_t, c)).then_inc(ld_x[c], 16)
            sp.dma_start(bv[:], bv_d.broadcast_to([P, D])).then_inc(ld_const, 16)
            sp.dma_start(bo[:], bo_d.broadcast_to([P, D])).then_inc(ld_const, 16)

            def send_parts(k):
                c, ct = k // 4, k % 4
                sp.wait_ge(ql_done, k + 1)
                unit = (c // 2) * GROUPS + (ct % 2) * 2
                sp.dma_start(parts_d[ct // 2, unit:unit + 2, c % 2].rearrange("u r a t -> u r (a t)"),
                             stage[:, k % QBUF].rearrange("p a t -> p (a t)")).then_inc(part_out[k % QBUF], 16)

            def load_stack(unit, slot, loads=range(STACK_LOADS)):
                for load in loads:
                    which, n = load // len(Q_PART), load % len(Q_PART)
                    stack, part = ((qs, Q_PART[n]), (ks, K_PART[n]))[which]
                    src = parts_d[which, bass.ds(unit, 1), :, :, part, :].rearrange("u s g t -> (u s g) t")
                    sp.dma_start(stack[n * HD:(n + 1) * HD, slot].rearrange("r s h t -> r (s h) t"),
                                 src.rearrange("(g r) t -> r g t", r=HD)).then_inc(stack_in[slot], 16)

            def load_max_rows(items, slot, half):
                sp.wait_ge(ring_free, items)
                sp.dma_start(qs[SROWS:MROWS, slot, half].rearrange("p h (t q) -> p (h t) q", q=P), mt[:, half, :]
                             ).then_inc(mrow_in[half], 16)

            for k in range(2 * NC + 2):
                send_parts(k)
            for n in range(QBUF):
                sp.wait_ge(part_out[n], sent(2 * NC, n))
            sp.wait_ge(wsplit_lo, 2)
            sp.wait_ge(w2_lo, NH // 2)
            sp.wait_ge(w13_lo, 2 * WSPLIT)
            for k in range(2 * NC + 2, 4 * NC):
                n = k - (2 * NC + 2)
                load_stack(0, 0, range(STACK_LOADS)[4 * n:4 * n + 4])
                send_parts(k)
            load_stack(1, 1)
            for n in range(QBUF):
                sp.wait_ge(part_out[n], sent(4 * NC, n))
            for half in range(2):
                load_max_rows(FIRST_ITEMS.index(("mt", half, 0, 0)) + 1, 0, half)

            def body(unit, par, more):
                load_max_rows(ring_count(unit, ("mt", 0, 0, 0)), 1 - par, 0)
                if more:
                    sp.wait_ge(s_ps, (unit + 1) * (2 * NSTEP))
                    load_stack(unit + 2, par)
                load_max_rows(ring_count(unit, ("mt", 1, 0, 0)), 1 - par, 1)

            with sp.Fori(0, UNITS // 2 - 1) as it:
                body(it * 2, 0, True)
                body(it * 2 + 1, 1, True)
            body(UNITS - 2, 0, False)

            for c in range(NC):
                sp.wait_ge(res_added, RES["FF2"] + c + 1)
                sp.dma_start(chunk_of(out_d.rearrange("(t p) n -> p t n", p=P), c), chunk_of(x, c)
                             ).then_inc(out_sent, 16)
            sp.wait_ge(out_sent, 16 * NC)

        @block.tensor
        def _(pe):
            PASSES = ((0, 0), (0, 1), (1, 0))

            def transposes(fill, src, ready):
                ready()
                if not isinstance(fill, int) or fill > 0:
                    pe.wait_ge(xt_hi, fill)
                    pe.wait_ge(xt_lo, fill)
                for d in range(ND):
                    for t in range(TPC):
                        last = nc.tensor.transpose(ps_t[:, d, t * P:(t + 1) * P], src(t, d), ident[:])
                last.then_inc(xt_ps, 1)

            def norm_transposes(kind, c):
                n = norm_no(kind, c)
                transposes(fill_no(kind, c), lambda t, d: xn[:, t, d * P:(d + 1) * P],
                           lambda: pe.wait_ge(xn_done, n + 1))

            def up(k, c, hc):
                for ps, w, freed, done in ((ps_gate, w1, silu_done, gate_done), (ps_lin, w3, u_done, lin_done)):
                    if not isinstance(k, int) or k >= 2:
                        pe.wait_ge(freed, k - 1)
                    n = 0
                    for d in range(ND):
                        for wp, xp in PASSES:
                            last = nc.tensor.matmul(ps[hc % 2][:], w[:, wp, d, hc * P:(hc + 1) * P],
                                                    xt[:, bass.ds(c, 1), xp, d, :].rearrange("p o t -> p (o t)"),
                                                    start=n == 0, stop=n == 5)
                            n += 1
                    last.then_inc(done, 1)

            def down(k, hc, chunks_before):
                pe.wait_ge(ul_done, k + 1)
                if hc == 0 and (not isinstance(chunks_before, int) or chunks_before > 0):
                    pe.wait_ge(res_added, chunks_before)
                for t in range(TPC):
                    for n, (wp, up_) in enumerate(PASSES):
                        lhs = (uh, ul)[up_]
                        last = nc.tensor.matmul(ps_down[:, t // 2, (t % 2) * D:(t % 2 + 1) * D],
                                                lhs[:, hc % 2, t * P:(t + 1) * P], w2[:, wp, hc, :],
                                                start=hc == 0 and n == 0 and t % 2 == 0,
                                                stop=hc == NH - 1 and n == 2, skip_group_check=True)
                last.then_inc(down_done if hc == NH - 1 else down_used, 1)

            def feed_forward(layer, fills, c, before, extra):
                k0 = (layer * NC + c) * NH
                res = (RES["FF"], RES["FF2"])[layer] + c
                pe.wait_ge(xt_lo, fills)
                pe.wait_ge(xt_hi, fills)
                for hc in range(NH):
                    up(k0 + hc, c, hc)
                    if hc == 0:
                        before()
                    else:
                        down(k0 + hc - 1, hc - 1, res)
                    extra(hc)

            def last_down(layer, c):
                down((layer * NC + c) * NH + NH - 1, NH - 1, 0)

            pe.wait_ge(ld_const, 16 * 9)
            norm_transposes("IN", 0)

            def hadamard(i):
                if i == 0:
                    pe.wait_ge(fly_sum, 3)
                    pe.wait_ge(fly_diff, 3)
                if i >= 2:
                    pe.wait_ge(w2_lo, i - 1)
                nc.tensor.matmul(ps_down[:, i % 2, :], had[:], fly_out(i),
                                 start=True, stop=True).then_inc(had_ps, 1)

            def first_extra(hc):
                if hc < 2:
                    hadamard(2 * hc)
                    hadamard(2 * hc + 1)
                if hc == 1:
                    pe.wait_ge(w2_lo, NH // 2)
                    pe.wait_ge(w2_hi, NH // 2)
                if hc in (2, 4, 6):
                    norm_transposes("IN", hc // 2)

            pe.wait_ge(xt_lo, 1)
            pe.wait_ge(xt_hi, 1)
            for hc in range(NH):
                if hc % 2 == 0:
                    pe.wait_ge(w13_lo, hc + 2)
                    pe.wait_ge(w13_hi, hc + 2)
                up(hc, 0, hc)
                first_extra(hc)
                if hc >= 1:
                    down(hc - 1, hc - 1, 0)

            with pe.Fori(1, NC) as c:
                feed_forward(0, fill_no("IN", c) + 1, c, lambda: last_down(0, c - 1),
                             lambda hc: norm_transposes("FF", c - 1) if hc == 3 else None)
            last_down(0, NC - 1)

            pe.wait_ge(silu_done, NC * NH)
            pe.wait_ge(u_done, NC * NH)
            pe.wait_ge(wsplit_lo, 2)
            for c in range(NC):
                pe.wait_ge(xt_lo, fill_no("FF", c) + 1)
                pe.wait_ge(xt_hi, fill_no("FF", c) + 1)
                for ct in range(4):
                    k = 4 * c + ct
                    if k >= 2:
                        pe.wait_ge(qf_done, k - 1)
                    for n, (d, (wp, xp)) in enumerate([(d, p) for d in range(ND) for p in PASSES]):
                        last = nc.tensor.matmul(banks[k % 2][:], wqkv[:, wp, d, ct * P:(ct + 1) * P],
                                                xt[:, c, xp, d, :], start=n == 0, stop=n == 5)
                    last.then_inc(qk_ps, 1)
                for vv in range(2):
                    i = 2 * c + vv
                    if i >= 2:
                        pe.wait_ge(v_done, i - 1)
                    for tt in range(2):
                        t = 2 * vv + tt
                        for n, (d, (wp, xp)) in enumerate([(d, p) for d in range(ND) for p in PASSES]):
                            last = nc.tensor.matmul(banks[2 + i % 2][:, tt * D:(tt + 1) * D],
                                                    xt[:, c, xp, d, t * P:(t + 1) * P], wqkv[:, wp, d, 2 * D:3 * D],
                                                    start=tt == 0 and n == 0, stop=n == 5, skip_group_check=True)
                    last.then_inc(v_ps, 1)
                if c == 0:
                    norm_transposes("FF", NC - 1)

            def suffix_sums(i):
                if i < KT - 2:
                    pe.wait_ge(suf_done, KT - 2 - i)
                    pe.wait_ge(wsum_done, KT - 2 - i)
                rest = {KT - 1: None, KT - 2: v_all[:, KT - 1]}.get(i, w_sum(i))
                out = ps_down[:, i % 2, :].rearrange("p (u n) -> p u n", u=UNITS)
                last = nc.tensor.matmul(out, after[:], v_all[:, i], start=True, stop=rest is None)
                if rest is not None:
                    last = nc.tensor.matmul(out, ones[:], rest, start=False, stop=True)
                last.then_inc(suf_ps, 1)

            def ring_item(item, bank, free_at, unit, par, prev_unit):
                kind, a, h, piece = item
                out = ps_ring[bank]
                if free_at is not None:
                    pe.wait_ge(ring_free, free_at)
                if kind == "red":
                    n = red_width(a, piece)
                    diagonal = piece == a // TPC
                    last = nc.tensor.matmul(out[:, 0:n], qs[0:SROWS, par, a // TPC, h, (a % TPC) * P:(a % TPC + 1) * P],
                                            ks[0:SROWS, par, piece, h, 0:n], start=True, stop=not diagonal)
                    if diagonal:
                        last = nc.tensor.matmul(out[:, n - P:n], ident_b[:], tri_b[:], start=False, stop=True)
                elif kind == "mt":
                    loop_wait(pe, mp_cut, unit * 2 + a + 1)
                    last = nc.tensor.transpose(out[0:PARTS * MT, 0:P // 2].bitcast(BF16),
                                               mpart[:, a].rearrange("p c h t -> p (c h t)"), ident_b[:])
                else:
                    pe.wait_ge(o_copied, prev_unit * 2 + a + 1)
                    for t in range(TPC):
                        last = nc.tensor.transpose(out[:, t * P:(t + 1) * P], o_raw[:, t * P:(t + 1) * P], ident[:])
                last.then_inc(ring_full, 1)

            def scores(step, s, p, par, unit):
                c, j, q0 = STEPS[s]
                if p == 0 and s in (0, STEPS_C0):
                    pe.wait_ge(mrow_in[c], (unit + 1) * 16)
                if not isinstance(step, int) or step > 0:
                    pe.wait_ge(p_done, step * 2 - 1 + p)
                for hh in range(2):
                    h = 2 * p + hh
                    last = nc.tensor.matmul(ps_s[p][:, hh, 0:CH - q0], ks[:, par, j // TPC, h, (j % TPC) * P:(j % TPC + 1) * P],
                                            qs[:, par, c, h, q0:CH], start=True, stop=True)
                last.then_inc(s_ps, 1)

            def values(step, s, par, unit):
                c, j, q0 = STEPS[s]
                pe.wait_ge(p_done, step * 2 + 2)
                if s in DIAG:
                    pe.wait_ge(p_masked, unit * len(DIAG) + (DIAG.index(s) + 1))
                if s == 0:
                    pe.wait_ge(vg_done, unit + 1)
                if s in (0, STEPS_C0) and (not isinstance(unit, int) or unit * 2 + c > 0):
                    pe.wait_ge(o_copied, unit * 2 + c)
                for h in range(GH):
                    last = nc.tensor.matmul(ps_o[VW * h:VW * (h + 1), q0:CH], vg[:, par, j, h, :],
                                            probs[:, s % RING, h, 0:CH - q0], start=j == 0,
                                            stop=j * P == (c + 1) * CH - P, tile_position=(0, VW * h),
                                            skip_group_check=True)
                last.then_inc(pv_done, 1)

            def first_scores(s):
                for p in range(2):
                    scores(s, s, p, 0, 0)
                if s > 0:
                    values(s - 1, s - 1, 0, 0)

            pe.wait_ge(qf_done, 4 * NC)
            pe.wait_ge(v_done, 2 * NC)
            pe.wait_ge(stack_ones, 1)
            pe.wait_ge(stack_in[0], 16 * STACK_LOADS)
            for n, item in enumerate(FIRST_ITEMS):
                if n == FIRST_SCORES:
                    pe.wait_ge(suf_done, KT)
                if n >= FIRST_SCORES and (n - FIRST_SCORES) % FIRST_GAP == 0 and (n - FIRST_SCORES) // FIRST_GAP < AHEAD:
                    first_scores((n - FIRST_SCORES) // FIRST_GAP)
                ring_item(item, (n + 2) % RING, n - 2 if n >= RING else None, 0, 0, None)
                if n % 2 == 1 and SUFFIX_FROM <= n < SUFFIX_FROM + 2 * KT:
                    suffix_sums(KT - 1 - (n - SUFFIX_FROM) // 2)

            def body(unit, par, visit, last):
                ring0 = NFIRST + unit * NBODY
                pos = 0
                if not last:
                    pe.wait_ge(stack_in[1 - par], visit * (16 * STACK_LOADS))
                for t in range(NSTEP if not last else NSTEP - AHEAD):
                    s = (AHEAD + t) % NSTEP
                    step = unit * NSTEP + (AHEAD + t)
                    here = t < NSTEP - AHEAD
                    items = BODY[t] if not last else [i for i in BODY[t] if i[0] == "ot"]
                    for p in range(2):
                        scores(step, s, p, par if here else 1 - par, unit if here else unit + 1)
                        for item in items[p * len(items) // 2:(p + 1) * len(items) // 2]:
                            if last:
                                free_at = ring0 + pos
                            else:
                                free_at = ring0 + (pos - 2 if pos >= RING else (0, -2, -1)[pos])
                            ring_item(item, pos % RING, free_at, unit + 1, 1 - par, unit)
                            pos += 1
                    was_here = t - 1 < NSTEP - AHEAD
                    values(step - 1, (s - 1) % NSTEP, par if was_here else 1 - par, unit if was_here else unit + 1)
                if last:
                    values(UNITS * NSTEP - 1, NSTEP - 1, par, unit)
                    ring_item(("ot", 1, 0, 0), pos % RING, ring0 + pos, unit, par, unit)

            with pe.Fori(0, UNITS // 2 - 1) as it:
                body(it * 2, 0, it + 1, False)
                body(it * 2 + 1, 1, it + 2, False)
            body(UNITS - 2, 0, UNITS // 2, False)
            body(UNITS - 1, 1, None, True)

            def att_transposes(c):
                b, j0 = c // 2, (c % 2) * TPC
                transposes(fill_no("AT", c),
                           lambda t, d: o_tok[:, j0 + t, b * GROUPS + 2 * d:b * GROUPS + 2 * d + 2, :].rearrange("p g n -> p (g n)"),
                           lambda: pe.wait_ge(o_done, (b + 1) * GROUPS * 2 + c % 2))

            pe.wait_ge(p_done, 2 * NSTEP * UNITS)
            att_transposes(0)
            for c in range(NC):
                if c + 1 < NC:
                    att_transposes(c + 1)
                pe.wait_ge(xt_lo, fill_no("AT", c) + 1)
                pe.wait_ge(xt_hi, fill_no("AT", c) + 1)
                pe.wait_ge(res_added, RES["OUT"] + c)
                for t in range(TPC):
                    for n, (d, (wp, xp)) in enumerate([(d, p) for d in range(ND) for p in PASSES]):
                        last = nc.tensor.matmul(ps_down[:, t // 2, (t % 2) * D:(t % 2 + 1) * D],
                                                xt[:, c, xp, d, t * P:(t + 1) * P], wo[:, wp, d, :],
                                                start=n == 0 and t % 2 == 0, stop=n == 5, skip_group_check=True)
                last.then_inc(down_done, 1)
                if c >= 1:
                    norm_transposes("OUT", c - 1)
            pe.wait_ge(ring_free, RING_TOTAL)

            feed_forward(1, fill_no("OUT", 0) + 1, 0, lambda: None,
                         lambda hc: norm_transposes("OUT", NC - 1) if hc == 0 else None)
            with pe.Fori(1, NC) as c:
                feed_forward(1, len(FILLS), c, lambda: last_down(1, c - 1), lambda hc: None)
            last_down(1, NC - 1)

        @block.scalar
        def _(act):
            act.dma_start(w3_raw[:], w3t_d.rearrange("(c p) n -> p c n", p=P)).then_inc(ld_w3, 16)
            act.dma_start(wqkv_raw[:], wqkv_d.rearrange("(c p) n -> p c n", p=P)).then_inc(ld_wqkv, 16)
            act.dma_start(wo_raw[:], wo_d.rearrange("(c p) n -> p c n", p=P)).then_inc(ld_wo, 16)

            def fill_hi(kind, c):
                act.wait_ge(xt_ps, fill_no(kind, c) + 1)
                for d in range(ND):
                    last = nc.scalar.copy(xt[:, bass.ds(c, 1), 0, d, :].rearrange("p o t -> p (o t)"), ps_t[:, d, :])
                last.then_inc(xt_hi, 1)

            for n in range(2 * WSPLIT):
                w, raw, loaded = ((w1, w1_raw, ld_w1), (w3, w3_raw, ld_w3))[n % 2]
                act.wait_ge(loaded, 16)
                cols = slice((n // 2) * WP, (n // 2 + 1) * WP)
                nc.scalar.copy(w[:, 0, :, cols], raw[:, :, cols]).then_inc(w13_hi, 1)
                if n == 1:
                    fill_hi("IN", 0)

            def gate(k, hc):
                act.wait_ge(gate_done, k + 1)
                if not isinstance(k, int) or k >= 2:
                    act.wait_ge(ul_done, k - 1)
                nc.scalar.activation(u[:, hc % 2, :], ps_gate[hc % 2][:], ACT.Silu).then_inc(silu_done, 1)

            def hidden_hi(k, hc, downs):
                act.wait_ge(u_done, k + 1)
                if downs is not None:
                    downs()
                nc.scalar.copy(uh[:, hc % 2, :], u[:, hc % 2, :]).then_inc(uh_done, 1)

            def downs_before(eng, layer, c, hc):
                if hc >= 2:
                    eng.wait_ge(down_used, (layer * NC + c) * (NH - 1) + hc - 1)
                elif isinstance(c, int) and c == 0 and layer == 0:
                    return
                elif hc == 0:
                    eng.wait_ge(down_used, (layer * NC + c) * (NH - 1))
                else:
                    eng.wait_ge(down_done, c + (RES["FF"], RES["FF2"])[layer])

            def feed_forward(layer, c, extra):
                for hc in range(NH):
                    k = (layer * NC + c) * NH + hc
                    gate(k, hc)
                    hidden_hi(k, hc, lambda: downs_before(act, layer, c, hc))
                    extra(hc)

            def w2_part(i):
                act.wait_ge(had_ps, i + 1)
                nc.scalar.activation(w2[:, 0, 2 * i:2 * i + 2, :], ps_down[:, i % 2, :].rearrange("p (a n) -> p a n", a=2),
                                     ACT.Copy, scale=W2_SCALE).then_inc(w2_hi, 1)

            for hc in range(NH):
                gate(hc, hc)
                if hc < 2:
                    w2_part(2 * hc)
                    w2_part(2 * hc + 1)
                hidden_hi(hc, hc, lambda: downs_before(act, 0, 0, hc))
                if hc in (2, 4, 6):
                    fill_hi("IN", hc // 2)

            with act.Fori(1, NC) as c:
                feed_forward(0, c, lambda hc: fill_hi("FF", c - 1) if hc == 3 else None)

            act.wait_ge(ld_const, 16 * 9)
            def middle_part(k):
                act.wait_ge(r1_done, k + 1)
                nc.scalar.copy(stage[:, k % QBUF, 1, :], r1[:, k % 2, :]).then_inc(qm_done, 1)

            for k in range(4 * NC):
                if k == LAST_FILL:
                    fill_hi("FF", NC - 1)
                act.wait_ge(qk_ps, k + 1)
                if k >= 2:
                    act.wait_ge(r1_done, k - 1)
                nc.scalar.activation(qf[:, k % 2, :], banks[k % 2][:], ACT.Identity,
                                     bias=bqk[:, k % 4:k % 4 + 1]).then_inc(qf_done, 1)
                act.wait_ge(qf_done, k + 1)
                if k >= QBUF:
                    act.wait_ge(part_out[k % QBUF], sent(k - QBUF + 1, k % QBUF))
                nc.scalar.copy(stage[:, k % QBUF, 0, :], qf[:, k % 2, :]).then_inc(qh_done, 1)
                if k >= 1:
                    middle_part(k - 1)
            middle_part(4 * NC - 1)

            act.wait_ge(ql_done, 4 * NC)
            for n in range(QBUF):
                act.wait_ge(part_out[n], sent(4 * NC, n))
            for n in range(KT):
                act.wait_ge(suf_ps, n + 1)
                i = KT - 1 - n
                nc.scalar.copy(suffix[:, i], ps_down[:, i % 2, :].rearrange("p (u n) -> p u n", u=UNITS)
                               ).then_inc(suf_done, 1)

            def exponentials(step, s, p):
                c, j, q0 = STEPS[s]
                act.wait_ge(s_ps, step * 2 + p + 1)
                if p == 0 and (not isinstance(step, int) or step >= RING):
                    act.wait_ge(pv_done, step - (RING - 1))
                nc.scalar.activation(probs[:, s % RING, 2 * p:2 * p + 2, 0:CH - q0], ps_s[p][:, :, 0:CH - q0],
                                     ACT.Exp, scale=SCALE).then_inc(p_done, 1)

            def copy_o(unit, c):
                act.wait_ge(pv_done, unit * NSTEP + (STEPS_C0, NSTEP)[c])
                if c == 1:
                    act.wait_ge(ring_full, ring_count(unit, ("ot", 0, 0, 0)))
                elif not isinstance(unit, int) or unit > 0:
                    act.wait_ge(ring_full, (unit - 1) * NBODY + (NFIRST + BODY_ITEMS.index(("ot", 1, 0, 0)) + 1))
                nc.scalar.copy(o_raw[:], ps_o[:]).then_inc(o_copied, 1)

            for s in range(AHEAD):
                for p in range(2):
                    exponentials(s, s, p)

            def body(unit, par, last):
                for t in range(NSTEP if not last else NSTEP - AHEAD):
                    if t == 1:
                        act.wait_ge(ea_done, unit + 1)
                        nc.scalar.activation(et[:, par], ea[:], ACT.Exp).then_inc(et_done, 1)
                    for p in range(2):
                        exponentials(unit * NSTEP + (AHEAD + t), (AHEAD + t) % NSTEP, p)
                        if p == 0 and t == STEPS_C0 - AHEAD + 1:
                            copy_o(unit, 0)
                        if p == 0 and t == NSTEP - AHEAD + 1:
                            copy_o(unit, 1)
                if last:
                    copy_o(unit, 1)

            with act.Fori(0, UNITS // 2 - 1) as it:
                body(it * 2, 0, False)
                body(it * 2 + 1, 1, False)
            body(UNITS - 2, 0, False)
            body(UNITS - 1, 1, True)

            for kind, c in FILLS[2 * NC:-1]:
                fill_hi(kind, c)
            feed_forward(1, 0, lambda hc: fill_hi("OUT", NC - 1) if hc == 0 else None)
            with act.Fori(1, NC) as c:
                feed_forward(1, c, lambda hc: None)

        @block.vector
        def _(dve):
            def statistics(kind, c):
                n = norm_no(kind, c)
                if not isinstance(n, int) or n > 0:
                    loop_wait(dve, rstd_done, n)
                for t in range(TPC):
                    last = nc.vector.bn_stats(bn[:, t, :], x[:, bass.ds(c * TPC + t, 1), :].rearrange("p o n -> p (o n)"))
                last.then_inc(bn_done, 1)
                loop_wait(dve, bn_done, n + 1)
                for t in range(TPC):
                    last = nc.vector.bn_aggr(mv[:, t, :], bn[:, t, :])
                last.then_inc(mv_done, 1)

            def normalise(kind, c):
                n = norm_no(kind, c)
                dve.wait_ge(rstd_done, n + 1)
                if kind == "OUT":
                    dve.wait_ge(xt_ps, 2 * NC if c == 0 else fill_no(kind, c - 1) + 1)
                elif not isinstance(n, int) or n > 0:
                    dve.wait_ge(xt_ps, fill_no(kind, c))
                for t in range(TPC):
                    last = nc.vector.tensor_scalar(xn[:, t, :], x[:, bass.ds(c * TPC + t, 1), :].rearrange("p o n -> p (o n)"),
                                                   mv[:, t, 0:1], rstd[:, t:t + 1], ALU.subtract, ALU.mult)
                last.then_inc(xn_done, 1)

            def fill_lo(kind, c):
                dve.wait_ge(xt_hi, fill_no(kind, c) + 1)
                for d in range(ND):
                    view = [xt[:, bass.ds(c, 1), part, d, :].rearrange("p o t -> p (o t)") for part in range(2)]
                    last = nc.vector.tensor_tensor(view[1], ps_t[:, d, :], view[0].bitcast(F32), ALU.subtract)
                last.then_inc(xt_lo, 1)

            def add_residual(phase, c):
                dve.wait_ge(down_done, RES[phase] + c + 1)
                for i in range(2):
                    xc = x[:, bass.ds(c * TPC + 2 * i, 2), :]
                    last = nc.vector.tensor_tensor(xc, xc, ps_down[:, i, :].rearrange("p (a n) -> p a n", a=2), ALU.add)
                last.then_inc(res_added, 1)

            dve.wait_ge(ld_x[0], 16)
            statistics("IN", 0)
            normalise("IN", 0)
            dve.wait_ge(ld_const, 16 * 9)
            nc.vector.tensor_copy(ident_b[:], ident[:]).then_inc(const_cut, 1)
            nc.vector.tensor_copy(tri_b[:], tri_f[:]).then_inc(const_cut, 1)

            def butterflies(stage_no):
                if stage_no:
                    dve.wait_ge(fly_diff, stage_no)
                    dve.wait_ge(fly_sum, stage_no)
                else:
                    dve.wait_ge(ld_w2, 16)
                a, b, s_, _ = fly_views(stage_no)
                nc.vector.tensor_tensor(s_, a, b, ALU.add).then_inc(fly_sum, 1)

            for n in range(2 * WSPLIT):
                w, raw = ((w1, w1_raw), (w3, w3_raw))[n % 2]
                dve.wait_ge(w13_hi, n + 1)
                cols = slice((n // 2) * WP, (n // 2 + 1) * WP)
                nc.vector.tensor_tensor(w[:, 1, :, cols], raw[:, :, cols], w[:, 0, :, cols].bitcast(F32),
                                        ALU.subtract).then_inc(w13_lo, 1)
                if n == 1:
                    fill_lo("IN", 0)
                if n in (3, 5, 7):
                    butterflies((n - 3) // 2)

            def product(k, hc):
                dve.wait_ge(silu_done, k + 1)
                dve.wait_ge(lin_done, k + 1)
                nc.vector.tensor_tensor(u[:, hc % 2, :], u[:, hc % 2, :], ps_lin[hc % 2][:], ALU.mult
                                        ).then_inc(u_done, 1)

            def hidden_lo(k, hc):
                dve.wait_ge(uh_done, k + 1)
                nc.vector.tensor_tensor(ul[:, hc % 2, :], u[:, hc % 2, :], uh[:, hc % 2, :].bitcast(F32),
                                        ALU.subtract).then_inc(ul_done, 1)

            def w2_part(i):
                dve.wait_ge(w2_hi, i + 1)
                nc.vector.scalar_tensor_tensor(
                    w2[:, 1, 2 * i:2 * i + 2, :], ps_down[:, i % 2, :].rearrange("p (a n) -> p a n", a=2), W2_SCALE,
                    w2[:, 0, 2 * i:2 * i + 2, :].bitcast(F32), ALU.mult, ALU.subtract).then_inc(w2_lo, 1)

            for hc in range(NH):
                product(hc, hc)
                if hc < 2:
                    w2_part(2 * hc)
                    w2_part(2 * hc + 1)
                hidden_lo(hc, hc)
                if hc in (1, 3, 5):
                    c = (hc + 1) // 2
                    dve.wait_ge(ld_x[c], 16)
                    statistics("IN", c)
                    normalise("IN", c)
                if hc in (2, 4, 6):
                    fill_lo("IN", hc // 2)

            def feed_forward(layer, c, extra):
                for hc in range(NH):
                    k = (layer * NC + c) * NH + hc
                    product(k, hc)
                    hidden_lo(k, hc)
                    extra(hc)

            def tail(phase, norm, c):
                def extra(hc):
                    if hc == 0:
                        add_residual(phase, c)
                    if norm and hc == 1:
                        dve.wait_ge(res_added, RES[phase] + c + 1)
                        statistics(norm, c)
                    if norm and hc == 2:
                        normalise(norm, c)
                    if norm and hc == 3:
                        fill_lo(norm, c)
                return extra

            with dve.Fori(1, NC) as c:
                feed_forward(0, c, tail("FF", "FF", c - 1))

            def values_in(i):
                dve.wait_ge(v_ps, i + 1)
                b, j = i // 4, 2 * (i % 4)
                for tt in range(2):
                    last = nc.vector.tensor_tensor(
                        v_all[:, j + tt, b * GROUPS:(b + 1) * GROUPS, :],
                        banks[2 + i % 2][:, tt * D:(tt + 1) * D].rearrange("p (g n) -> p g n", g=GROUPS),
                        bv[:].rearrange("p (g n) -> p g n", g=GROUPS), ALU.add)
                last.then_inc(v_done, 1)

            def last_part(k):
                dve.wait_ge(qm_done, k + 1)
                nc.vector.tensor_tensor(stage[:, k % QBUF, 2, :], r1[:, k % 2, :], stage[:, k % QBUF, 1, :],
                                        ALU.subtract).then_inc(ql_done, 1)

            end = tail("FF", "FF", NC - 1)
            end(0)
            for k in range(4 * NC):
                dve.wait_ge(qh_done, k + 1)
                if k >= 2:
                    dve.wait_ge(qm_done, k - 1)
                    dve.wait_ge(ql_done, k - 1)
                nc.vector.tensor_tensor(r1[:, k % 2, :], qf[:, k % 2, :], stage[:, k % QBUF, 0, :], ALU.subtract
                                        ).then_inc(r1_done, 1)
                if k >= 1:
                    last_part(k - 1)
                if k < 2:
                    end(k + 1)
                if k == LAST_FILL - 1:
                    end(3)
                if k % 4 == 3:
                    values_in(2 * (k // 4))
                    values_in(2 * (k // 4) + 1)
            last_part(4 * NC - 1)

            def ring_item(item, bank, after_count, unit, par, prev_unit, prev_par):
                kind, a, h, piece = item
                dve.wait_ge(ring_full, after_count)
                src = ps_ring[bank]
                if kind == "red":
                    at = RED_A.index(item) if a < TPC else NA + RED_B.index(item)
                    nc.vector.reduce_max(mp[:, at:at + 1], src[:, 0:red_width(a, piece)], AX.X).then_inc(ring_free, 1)
                    if item == RED_B[-1]:
                        dve.wait_ge(ring_free, after_count)
                        two = mp[:, NA:NA + NB].rearrange("p (i c h) -> p c h i", c=2, h=GH)
                        nc.vector.tensor_tensor(mb[:], two[:, 0], two[:, 1], ALU.max).then_inc(mb_done, 1)
                        dve.wait_ge(mb_done, unit + 1)
                        nc.vector.scalar_tensor_tensor(mneg[:, par, :, TPC:KT], mb[:], -1.0, neg_floor[:],
                                                       ALU.mult, ALU.min).then_inc(mneg_done, 1)
                elif kind == "mt":
                    if not isinstance(unit, int) or unit > 0:
                        dve.wait_ge(mrow_in[a], unit * 16)
                    nc.vector.tensor_copy(mt[:, a, :], src[0:PARTS * MT, 0:P // 2].bitcast(BF16)).then_inc(ring_free, 1)
                else:
                    oc = prev_unit * 2 + a
                    cols = slice(a * TPC, (a + 1) * TPC)
                    four = src[:].rearrange("p (t h n) -> p t h n", t=TPC, h=GH)
                    dve.wait_ge(em_done, prev_unit + 1)
                    dve.wait_ge(o_done, oc + 1)
                    nc.vector.tensor_tensor(dsum[:], four[:, :, :, HD], ecnt[:, prev_par, :, cols].rearrange("p h t -> p t h"),
                                            ALU.add).then_inc(dsum_done, 1)
                    nc.vector.tensor_tensor(num[:], four[:, :, :, 0:HD], em[:, prev_par, cols], ALU.add
                                            ).then_inc(ring_free, 1)
                    dve.wait_ge(dsum_done, oc + 1)
                    nc.vector.reciprocal(rcp[:], dsum[:]).then_inc(rcp_done, 1)

            for n, item in enumerate(FIRST_ITEMS):
                ring_item(item, (n + 2) % RING, n + 1, 0, 0, None, None)

            def body(unit, par, last):
                ring0 = NFIRST + unit * NBODY
                items = BODY_ITEMS if not last else LAST_ITEMS
                for n, item in enumerate(items):
                    ring_item(item, n % RING, ring0 + n + 1, unit + 1, 1 - par, unit, par)

            with dve.Fori(0, UNITS // 2 - 1) as it:
                body(it * 2, 0, False)
                body(it * 2 + 1, 1, False)
            body(UNITS - 2, 0, False)
            body(UNITS - 1, 1, True)

            dve.wait_ge(bo_added, 1)
            def finish(c):
                add_residual("OUT", c)
                dve.wait_ge(res_added, RES["OUT"] + c + 1)
                statistics("OUT", c)
                normalise("OUT", c)

            for kind, c in FILLS[2 * NC:-1]:
                fill_lo(kind, c)
                if (kind, c) in (("AT", 1), ("OUT", 0), ("OUT", 1), ("OUT", 2)):
                    finish(0 if kind == "AT" else c + 1)
            feed_forward(1, 0, lambda hc: fill_lo("OUT", NC - 1) if hc == 0 else None)
            with dve.Fori(1, NC) as c:
                feed_forward(1, c, tail("FF2", None, c - 1))
            add_residual("FF2", NC - 1)

        @block.gpsimd
        def _(pool):
            nc.gpsimd.memset(neg_half[:], -0.5).then_inc(pool_const, 1)
            nc.gpsimd.memset(ones[:], 1.0).then_inc(pool_const, 1)

            def inverse_deviation(kind, c):
                n = norm_no(kind, c)
                loop_wait(pool, mv_done, n + 1)
                if not isinstance(n, int) or n > 0:
                    loop_wait(pool, xn_done, n)
                nc.gpsimd.tensor_scalar_add(ve[:], mv[:, :, 1], EPS).then_inc(ve_done, 1)
                loop_wait(pool, ve_done, n + 1)
                nc.gpsimd.tensor_tensor(rstd[:], ve[:], neg_half[:], ALU.pow).then_inc(rstd_done, 1)

            pool.wait_ge(pool_const, 2)
            inverse_deviation("IN", 0)
            for stage_no in range(3):
                if stage_no:
                    pool.wait_ge(fly_sum, stage_no)
                    pool.wait_ge(fly_diff, stage_no)
                else:
                    pool.wait_ge(ld_w2, 16)
                a, b, _, d_ = fly_views(stage_no)
                nc.gpsimd.tensor_tensor(d_, a, b, ALU.subtract).then_inc(fly_diff, 1)
            for c in range(1, NC):
                inverse_deviation("IN", c)
            for n, (w, raw, loaded) in enumerate(((wqkv, wqkv_raw, ld_wqkv), (wo, wo_raw, ld_wo))):
                pool.wait_ge(loaded, 16)
                nc.gpsimd.tensor_copy(w[:, 0], raw[:]).then_inc(wsplit_hi, 1)
                pool.wait_ge(wsplit_hi, n + 1)
                nc.gpsimd.tensor_tensor(w[:, 1], raw[:], w[:, 0].bitcast(F32), ALU.subtract).then_inc(wsplit_lo, 1)
                pool.wait_ge(wsplit_lo, n + 1)
            with pool.Fori(1, NC) as c:
                inverse_deviation("FF", c - 1)
            pool.wait_ge(w13_lo, 2 * WSPLIT)
            pool.wait_ge(w2_lo, NH // 2)
            pool.wait_ge(rstd_done, 2 * NC - 1)
            nc.gpsimd.memset(ks[SROWS:MROWS], 1.0).then_inc(stack_ones, 1)
            pool.wait_ge(stack_ones, 1)
            inverse_deviation("FF", NC - 1)
            pool.wait_ge(ld_const, 16 * 9)
            for c in range(NC):
                pool.wait_ge(xn_done, norm_no("FF", c) + 1)
                last = nc.gpsimd.tensor_tensor(chunk_of(x, c), chunk_of(x, c), bo[:].unsqueeze(1).broadcast_to([P, TPC, D]),
                                               ALU.add)
            last.then_inc(bo_added, 1)

            pool.wait_ge(down_done, NC)
            nc.gpsimd.memset(vg[:], 1.0).then_inc(vg_ones, 1)
            nc.gpsimd.memset(num[:], 0.0).then_inc(o_done, 1)
            pool.wait_ge(v_done, 2 * NC)
            pool.wait_ge(vg_ones, 1)

            def take_values(unit, par):
                if not isinstance(unit, int) or unit >= 1:
                    loop_wait(pool, pv_done, (unit - 1) * NSTEP + 1)
                nc.gpsimd.tensor_copy(vg[:, par, :, :, 0:HD],
                                      v_all[:, :, bass.ds(unit, 1)].rearrange("p j o (h n) -> p (j o) h n", h=GH)
                                      ).then_inc(vg_done, 1)

            pool.wait_ge(xt_ps, 2 * NC)
            for n in range(1, KT - 1):
                i = KT - 2 - n
                first = v_all[:, KT - 1] if n == 1 else w_sum(i + 1)
                if n > 1:
                    pool.wait_ge(wsum_done, n - 1)
                if n > 2:
                    pool.wait_ge(suf_ps, n)
                nc.gpsimd.tensor_tensor(w_sum(i), first, v_all[:, i + 1], ALU.add).then_inc(wsum_done, 1)
            take_values(0, 0)

            def cut_maxima(unit, par, half):
                m = mneg[:, par, :, half * TPC:(half + 1) * TPC]
                base = unit * sum(CUTS) + half * CUTS[0]
                if half == 0:
                    if isinstance(unit, int) and unit == 0:
                        pool.wait_ge(ring_free, NA)
                    else:
                        loop_wait(pool, ring_free, ring_count(unit - 1, RED_A[-1]))
                    nc.gpsimd.tensor_scalar(m, mp[:, 0:NA].rearrange("p (i h) -> p h i", h=GH), MASKED / SCALE, -1.0,
                                            ALU.max, ALU.mult).then_inc(cut_step, 1)
                    base = base + 1
                    loop_wait(pool, cut_step, base)
                else:
                    loop_wait(pool, mneg_done, unit + 1)
                nc.gpsimd.tensor_copy(mpart[:, half, 0], m).then_inc(cut_step, 1)
                loop_wait(pool, cut_step, base + 1)
                nc.gpsimd.tensor_tensor(mres[:, half], m, mpart[:, half, 0], ALU.subtract).then_inc(cut_step, 1)
                loop_wait(pool, cut_step, base + 2)
                nc.gpsimd.tensor_copy(mpart[:, half, 1], mres[:, half]).then_inc(cut_step, 1)
                loop_wait(pool, cut_step, base + 3)
                nc.gpsimd.tensor_tensor(mpart[:, half, 2], mres[:, half], mpart[:, half, 1], ALU.subtract
                                        ).then_inc(mp_cut, 1)
                loop_wait(pool, mp_cut, unit * 2 + half + 1)

            def mask(step, s):
                loop_wait(pool, p_done, step * 2 + 2)
                tile = probs[:, s % RING, :, 0:P]
                nc.gpsimd.affine_select(out=tile, in_=tile, compare_op=ALU.is_ge, fill=0.0, base=0,
                                        pattern=[[0, GH], [1, P]], channel_multiplier=-1).then_inc(p_masked, 1)

            def masked_share(unit, par):
                nc.gpsimd.tensor_scalar(ea[:], mneg[:, par], SCALE, -MASKED, ALU.mult, ALU.min).then_inc(ea_step, 1)
                loop_wait(pool, ea_step, unit * 2 + 1)
                nc.gpsimd.tensor_scalar_add(ea[:], ea[:], MASKED).then_inc(ea_done, 1)
                loop_wait(pool, et_done, unit + 1)
                nc.gpsimd.tensor_tensor(ecnt[:, par], et[:, par], count[:].unsqueeze(1).broadcast_to([P, GH, KT]),
                                        ALU.mult).then_inc(ea_step, 1)
                loop_wait(pool, ea_step, unit * 2 + 2)
                nc.gpsimd.tensor_tensor(
                    em[:, par], suffix[:, :, bass.ds(unit, 1)].rearrange("p j o (h n) -> p (j o) h n", h=GH),
                    et[:, par].rearrange("p h t -> p t h").unsqueeze(3).broadcast_to([P, KT, GH, HD]),
                    ALU.mult).then_inc(em_done, 1)

            def scale_o(unit, c):
                oc = unit * 2 + c
                loop_wait(pool, rcp_done, oc + 1)
                nc.gpsimd.tensor_tensor(
                    o_tok[:, c * TPC:(c + 1) * TPC, bass.ds(unit, 1)].rearrange("p j o (h n) -> p (j o) h n", h=GH),
                    num[:], rcp[:].unsqueeze(3).broadcast_to([P, TPC, GH, HD]), ALU.mult).then_inc(o_done, 1)

            cut_maxima(0, 0, 0)
            for s in range(AHEAD):
                if s == AHEAD - 1:
                    cut_maxima(0, 0, 1)
                if s in DIAG:
                    mask(s, s)
            pool.wait_ge(suf_done, KT)

            def body(unit, par, last):
                for t in range(NSTEP if not last else NSTEP - AHEAD):
                    s = (AHEAD + t) % NSTEP
                    if t == NSTEP - 1:
                        cut_maxima(unit + 1, 1 - par, 1)
                    if s in DIAG:
                        mask(unit * NSTEP + (AHEAD + t), s)
                    if t == 0:
                        masked_share(unit, par)
                        if not last:
                            take_values(unit + 1, 1 - par)
                    if t == 4:
                        if not last:
                            cut_maxima(unit + 1, 1 - par, 0)
                        scale_o(unit, 0)
                scale_o(unit, 1)

            with pool.Fori(0, UNITS // 2 - 1) as it:
                body(it * 2, 0, False)
                body(it * 2 + 1, 1, False)
            body(UNITS - 2, 0, False)
            body(UNITS - 1, 1, True)

            for c in range(NC):
                inverse_deviation("OUT", c)


def constants():
    p = np.arange(P)
    bits = p[:, None] & p[None, :]
    odd = np.zeros((P, P), np.int64)
    for b in range(P.bit_length()):
        odd ^= (bits >> b) & 1
    floor = np.full((P, GH, KT // 2), -MASKED / SCALE, np.float32)
    floor[P - 1, :, KT // 2 - 1] = 3e38
    return {
        "had": (1.0 - 2.0 * odd).astype(np.float32),
        "ident": np.eye(P, dtype=np.float32),
        "tri": np.where(p[None, :] > p[:, None], NEG_BIG, 0.0).astype(np.float32),
        "after": (p[:, None] > p[None, :]).astype(np.float32),
        "count": (SEQ - 1 - (p[:, None] + P * np.arange(KT)[None, :])).astype(np.float32),
        "floor": floor,
    }


def kernel(L0_attn_x, L0_attn_Wqkv, L0_attn_bqkv, L0_attn_Wo, L0_attn_bo, L0_ffn_W1, L0_ffn_W2, L0_ffn_W3):
    import concourse.bacc as bacc
    from concourse.bass_utils import run_bass_kernel_spmd

    bqkv = np.asarray(L0_attn_bqkv)
    arrays = {
        "x": np.ascontiguousarray(np.asarray(L0_attn_x).reshape(TOKENS, D)),
        "w1t": np.ascontiguousarray(np.asarray(L0_ffn_W1).T),
        "w3t": np.ascontiguousarray(np.asarray(L0_ffn_W3).T),
        "w2t": np.ascontiguousarray(np.asarray(L0_ffn_W2).T),
        "wqkv": np.ascontiguousarray(np.asarray(L0_attn_Wqkv)),
        "wo": np.ascontiguousarray(np.asarray(L0_attn_Wo)),
        "bqk": np.ascontiguousarray(bqkv[:2 * D].reshape(4, P).T),
        "bv": np.ascontiguousarray(bqkv[2 * D:].reshape(1, D)),
        "bo": np.ascontiguousarray(np.asarray(L0_attn_bo).reshape(1, D)),
        **constants(),
    }
    nc = bacc.Bacc("TRN2", target_bir_lowering=False, num_devices=1)
    args = [nc.dram_tensor("in_" + n, a.shape, mybir.dt.from_np(a.dtype), kind="ExternalInput").ap() for n, a in arrays.items()]
    out = nc.dram_tensor("out_tokens", (TOKENS, D), F32, kind="ExternalOutput").ap()
    macaron(nc, *args, out)
    r = run_bass_kernel_spmd(nc, [{"in_" + n: a for n, a in arrays.items()}], core_ids=[0])
    return r.results[0]["out_tokens"].reshape(BATCH, SEQ, D)
```

```python
from contextlib import ExitStack

import numpy as np

import concourse.bass as bass
from concourse import mybir

F32 = mybir.dt.float32
F32R = mybir.dt.float32r
BF16 = mybir.dt.bfloat16
ACT = mybir.ActivationFunctionType
ALU = mybir.AluOpType
AX = mybir.AxisListType

P = 128
BATCH, SEQ, D = 2, 1024, 256
HIDDEN = 1024
HEADS, HD = 16, 16
TOKENS = BATCH * SEQ
CH = 512
NC = TOKENS // CH
TPC = CH // P
ND = D // P
NH = HIDDEN // P
GH = 4
GROUPS = HEADS // GH
UNITS = BATCH * GROUPS
KT = SEQ // P
VW = 32
PARTS = 3
Q_PART = (0, 0, 0, 1, 1, 2)
K_PART = (0, 1, 2, 0, 1, 0)
STACK_LOADS = len(Q_PART) + len(K_PART)
QBUF = 4
SROWS = 6 * HD
MROWS = SROWS + PARTS
EPS = 1e-5
SCALE = 1.0 / float(np.sqrt(HD))
MASKED = -10000.0
NEG_BIG = -1e30

STEPS = [(c, j, max(0, j * P - c * CH)) for c in range(2) for j in range(KT) if j * P < (c + 1) * CH]
NSTEP = len(STEPS)
STEPS_C0 = sum(1 for s in STEPS if s[0] == 0)
AHEAD = 3
DIAG = [s for s, (c, j, q0) in enumerate(STEPS) if j * P >= c * CH]

RED_A = [("red", i, h, 0) for i in range(KT // 2) for h in range(GH)]
RED_B = [("red", i, h, piece) for i in range(KT // 2, KT) for piece in range(2) for h in range(GH)]
NA, NB = len(RED_A), len(RED_B)
RING = 3


W2_SCALE = 0.5 / float(np.sqrt(HIDDEN))


def loop_wait(eng, sem, value):
    eng.wait_ge(sem, value)
    if not isinstance(value, int):
        eng.nop(nofuse=True)


def red_width(i, piece):
    return min(CH, (i + 1) * P - piece * CH)


def body_plan():
    reds = [(it, red_width(it[1], it[3]) + 120) for it in RED_A + RED_B]
    total = sum(w for _, w in reds)
    slots = [[] for _ in range(NSTEP)]
    spread = NSTEP - 1.0
    done = 0
    for n, (it, w) in enumerate(reds):
        at = min(NSTEP - 2, int(done * spread / total))
        slots[at].append(it)
        if n == NA + 3:
            slots[at].append(("mt", 0, 0, 0))
        done += w
    slots[STEPS_C0 - AHEAD + 2].append(("ot", 0, 0, 0))
    slots[NSTEP - AHEAD + 2] += [("ot", 1, 0, 0), ("mt", 1, 0, 0)]
    return slots


BODY = body_plan()
BODY_ITEMS = [it for s in BODY for it in s]
FIRST_ITEMS = RED_A + RED_B[:12] + [("mt", 0, 0, 0)] + RED_B[12:] + [("mt", 1, 0, 0)]
SUFFIX_FROM = 9
FIRST_GAP = 6
FIRST_SCORES = len(FIRST_ITEMS) - 1 - 2 * FIRST_GAP
LAST_ITEMS = [("ot", 0, 0, 0), ("ot", 1, 0, 0)]
NBODY, NFIRST = len(BODY_ITEMS), len(FIRST_ITEMS)
RING_TOTAL = NFIRST + (UNITS - 1) * NBODY + len(LAST_ITEMS)


def ring_count(unit, item):
    items = LAST_ITEMS if isinstance(unit, int) and unit == UNITS - 1 else BODY_ITEMS
    return unit * NBODY + (NFIRST + items.index(item) + 1)


def macaron(nc, x_d, w1t_d, w3t_d, w2t_d, wqkv_d, wo_d, bqk_d, bv_d, bo_d, had_d, ident_d, tri_d,
            after_d, count_d, floor_d, out_d):
    ctx = ExitStack()
    with ctx:
        def sb(name, shape, dt):
            return ctx.enter_context(nc.sbuf_tensor(name, shape, dt))

        def sem(name):
            return ctx.enter_context(nc.semaphore(name))

        x = sb("x", [P, NC * TPC, D], F32)
        w1 = sb("w1", [P, 2, ND, HIDDEN], F32R)
        w3 = sb("w3", [P, 2, ND, HIDDEN], F32R)
        w2 = sb("w2", [P, 2, NH, D], F32R)
        wo = sb("wo", [P, 2, ND, D], F32R)
        v_all = sb("v_all", [P, KT, UNITS, GH * HD], F32)

        def take_turns(*groups):
            made = []
            for g in groups[1:]:
                with ExitStack() as s:
                    made.append([s.enter_context(nc.sbuf_tensor(n, sh, t)) for n, sh, t in g])
            return [[sb(n, sh, t) for n, sh, t in groups[0]]] + made

        (xt,), (_, probs) = take_turns([("xt", [P, NC, 2, ND, CH], F32R)],
                                       [("xt_first", [P, 2, ND, CH], F32R), ("probs", [P, RING, GH, CH], F32)])
        (qs, ks), (w1_raw, w3_raw, w2_raw, wqkv_raw, wo_raw), (xa,) = take_turns(
            [("qs", [MROWS, 2, 2, GH, CH], BF16), ("ks", [MROWS, 2, 2, GH, CH], BF16)],
            [("w1_raw", [P, ND, HIDDEN], F32), ("w3_raw", [P, ND, HIDDEN], F32), ("w2_raw", [P, NH, D], F32),
             ("wqkv_raw", [P, ND, 3 * D], F32), ("wo_raw", [P, ND, D], F32)],
            [("xa", [P, 2, ND, CH], F32R)])
        (o_tok,), (wqkv, qf) = take_turns([("o_tok", [P, KT, UNITS, GH * HD], F32)],
                                          [("wqkv", [P, 2, ND, 3 * D], F32R), ("qf", [P, 2, CH], F32)])
        (u, uh, ul), (vg, o_raw, num) = take_turns(
            [("u", [P, 2, CH], F32), ("uh", [P, 2, CH], F32R), ("ul", [P, 2, CH], F32R)],
            [("vg", [P, 2, KT, GH, VW], F32), ("o_raw", [P, CH], F32), ("num", [P, TPC, GH, HD], F32)])
        (suffix,), (o_now,), (r1, stage) = take_turns(
            [("suffix", [P, KT, UNITS, GH * HD], F32)],
            [("o_now", [P, TPC, D], F32)],
            [("r1", [P, 2, CH], F32), ("stage", [P, QBUF, PARTS, CH], BF16)])
        xn = sb("xn", [P, TPC, D], F32)
        had = sb("had", [P, P], F32)
        ident = sb("ident", [P, P], F32)
        after = sb("after", [P, P], F32)
        ones = sb("ones", [P, P], F32)
        ident_b = sb("ident_b", [P, P], BF16)
        tri_f = sb("tri_f", [P, P], F32)
        tri_b = sb("tri_b", [P, P], BF16)
        bqk = sb("bqk", [P, 4], F32)
        bv = sb("bv", [P, D], F32)
        bo = sb("bo", [P, D], F32)
        count = sb("count", [P, KT], F32)
        neg_floor = sb("neg_floor", [P, GH, KT // 2], F32)
        bn = sb("bn", [P, TPC, 6], F32)
        mv = sb("mv", [P, TPC, 2], F32)
        ve = sb("ve", [P, TPC], F32)
        rstd = sb("rstd", [P, TPC], F32)
        neg_half = sb("neg_half", [P, TPC], F32)
        mp = sb("mp", [P, NA + NB], F32)
        mb = sb("mb", [P, GH, KT // 2], F32)
        mneg = sb("mneg", [P, 2, GH, KT], F32)
        mres = sb("mres", [P, 2, GH, KT // 2], F32)
        mpart = sb("mpart", [P, 2, PARTS, GH, KT // 2], BF16)
        MT = GH * KT // 2
        mt = sb("mt", [PARTS * MT, 2, P], BF16)
        ea = sb("ea", [P, GH, KT], F32)
        et = sb("et", [P, 2, GH, KT], F32)
        ecnt = sb("ecnt", [P, 2, GH, KT], F32)
        em = sb("em", [P, 2, KT, GH, HD], F32)
        dsum = sb("dsum", [P, TPC, GH], F32)
        rcp = sb("rcp", [P, TPC, GH], F32)

        banks = [ctx.enter_context(nc.psum_tensor(f"bank{i}", [P, CH], F32)) for i in range(4)]
        pair = [ctx.enter_context(nc.psum_tensor(f"pair{i}", [P, 2, CH], F32)) for i in range(2)]
        ps_gate, ps_lin = banks[0:2], banks[2:4]
        ps_down, ps_t = pair
        ps_ring, ps_o, ps_s = banks[0:3], banks[3], pair
        T_BANKS = [ps_t[:, d, :] for d in range(2)]
        FREE_BANKS = [t[:] for t in banks[1:3]]

        parts_d = nc.dram_tensor("parts", (2, UNITS, 2, GH * HD, PARTS, CH), BF16, kind="Internal").ap()

        ld_x = [sem(f"ld_x{c}") for c in range(NC)]
        ld_w1, ld_w3 = [[sem(f"ld_{w}_{i}") for i in range(2)] for w in ("w1", "w3")]
        ld_w2, ld_ident, ld_had = sem("ld_w2"), sem("ld_ident"), sem("ld_had")
        ld_wqkv, ld_wo, ld_const = sem("ld_wqkv"), sem("ld_wo"), sem("ld_const")
        const_cut, pool_const, stack_ones, vg_ones = sem("const_cut"), sem("pool_const"), sem("stack_ones"), sem("vg_ones")
        bn_done, mv_done, ve_done = sem("bn_done"), sem("mv_done"), sem("ve_done")
        rstd_done, xn_done = sem("rstd_done"), sem("xn_done")
        xt_ps, xt_hi, xt_lo = sem("xt_ps"), sem("xt_hi"), sem("xt_lo")
        w13_hi, w13_lo, fly_sum, fly_diff = sem("w13_hi"), sem("w13_lo"), sem("fly_sum"), sem("fly_diff")
        had_ps, w2_hi, w2_lo = sem("had_ps"), sem("w2_hi"), sem("w2_lo")
        wsplit_hi, wsplit_lo = sem("wsplit_hi"), sem("wsplit_lo")
        gate_done, lin_done, silu_done = sem("gate_done"), sem("lin_done"), sem("silu_done")
        u_done, uh_done, ul_done = sem("u_done"), sem("uh_done"), sem("ul_done")
        down_used, down_done, res_added = sem("down_used"), sem("down_done"), sem("res_added")
        qk_ps, qf_done, qh_done, r1_done = sem("qk_ps"), sem("qf_done"), sem("qh_done"), sem("r1_done")
        qm_done, ql_done, v_ps, v_done = sem("qm_done"), sem("ql_done"), sem("v_ps"), sem("v_done")
        part_out = [sem(f"part_out{i}") for i in range(QBUF)]
        stack_in = [sem(f"stack_in{i}") for i in range(2)]
        mrow_in = [sem(f"mrow_in{i}") for i in range(2)]
        wsum_done, suf_ps, suf_done = sem("wsum_done"), sem("suf_ps"), sem("suf_done")
        vg_done, bo_added, o_taken = sem("vg_done"), sem("bo_added"), sem("o_taken")
        at_ps, at_hi, at_lo, wo_done, att_added = (sem("at_ps"), sem("at_hi"), sem("at_lo"), sem("wo_done"),
                                                   sem("att_added"))
        ring_full, ring_free = sem("ring_full"), sem("ring_free")
        mb_done, mneg_done, cut_step, mp_cut = sem("mb_done"), sem("mneg_done"), sem("cut_step"), sem("mp_cut")
        ea_step, ea_done, et_done, em_done = sem("ea_step"), sem("ea_done"), sem("et_done"), sem("em_done")
        s_ps, p_done, p_masked, pv_done = sem("s_ps"), sem("p_done"), sem("p_masked"), sem("pv_done")
        o_copied, dsum_done, rcp_done, num_done, o_done = (sem("o_copied"), sem("dsum_done"), sem("rcp_done"),
                                                           sem("num_done"), sem("o_done"))
        out_sent = sem("out_sent")

        ORDER = {"IN": 0, "FF": NC, "OUT": 2 * NC}

        def fill_no(kind, c):
            return ORDER[kind] + c

        RES = {"FF": 0, "FF2": NC}
        WSPLIT = 4
        WP = HIDDEN // WSPLIT

        def chunk_of(t, c):
            return t[:, bass.ds(c * TPC, TPC), :]

        AT_SLOT, WO_SLOT, OUT_SLOT = 0, 2, 6
        LAST_FILL = 4
        CUTS = (4, 3)

        def fly_views(stage_no):
            fly = v_all[:, 0:NH // 2].rearrange("p j u n -> p (j u n)").rearrange("p (k n) -> p k n", n=D)
            places = (w2_raw[:], fly) if stage_no % 2 == 0 else (fly, w2_raw[:])
            src, dst = [t.rearrange("p (a two b) n -> p two a (b n)", two=2, b=1 << stage_no) for t in places]
            return src[:, 0], src[:, 1], dst[:, 0], dst[:, 1]

        def sent(projections, buf):
            return 16 * len(range(buf, projections, QBUF))

        def fly_out(i):
            return v_all[:, i].rearrange("p u n -> p (u n)")

        def w_sum(i):
            return xn[:, 2 * (i % 2):2 * (i % 2) + 2, :].rearrange("p a n -> p (a n)").rearrange("p (u n) -> p u n", u=UNITS)

        block = ctx.enter_context(nc.Block())

        @block.sync
        def _(sp):
            x_t = x_d.rearrange("(t p) n -> p t n", p=P)
            sp.dma_start(x[:, 0:TPC, :], x_t[:, 0:TPC, :]).then_inc(ld_x[0], 16)
            sp.dma_start(w2_raw[:], w2t_d.rearrange("(c p) n -> p c n", p=P)).then_inc(ld_w2, 16)
            sp.dma_start(ident[:], ident_d).then_inc(ld_ident, 16)
            for i in range(2):
                cols = slice(i * HIDDEN // 2, (i + 1) * HIDDEN // 2)
                for raw, w_d, loaded in ((w1_raw, w1t_d, ld_w1), (w3_raw, w3t_d, ld_w3)):
                    sp.dma_start(raw[:, :, cols], w_d.rearrange("(c p) n -> p c n", p=P)[:, :, cols]).then_inc(loaded[i], 16)
                if i == 0:
                    sp.dma_start(had[:], had_d).then_inc(ld_had, 16)
                    sp.dma_start(chunk_of(x, 1), chunk_of(x_t, 1)).then_inc(ld_x[1], 16)
            for c in range(2, NC):
                sp.dma_start(chunk_of(x, c), chunk_of(x_t, c)).then_inc(ld_x[c], 16)
            sp.dma_start(wqkv_raw[:], wqkv_d.rearrange("(c p) n -> p c n", p=P)).then_inc(ld_wqkv, 16)
            sp.dma_start(wo_raw[:], wo_d.rearrange("(c p) n -> p c n", p=P)).then_inc(ld_wo, 16)
            for t, d_ in ((bqk, bqk_d), (neg_floor, floor_d), (tri_f, tri_d), (after, after_d), (count, count_d),
                          (bv, bv_d.broadcast_to([P, D])), (bo, bo_d.broadcast_to([P, D]))):
                sp.dma_start(t[:], d_).then_inc(ld_const, 16)

            def send_parts(k):
                c, ct = k // 4, k % 4
                sp.wait_ge(ql_done, k + 1)
                unit = (c // 2) * GROUPS + (ct % 2) * 2
                sp.dma_start(parts_d[ct // 2, unit:unit + 2, c % 2].rearrange("u r a t -> u r (a t)"),
                             stage[:, k % QBUF].rearrange("p a t -> p (a t)")).then_inc(part_out[k % QBUF], 16)

            def load_stack(unit, slot, loads=range(STACK_LOADS)):
                for load in loads:
                    which, n = load // len(Q_PART), load % len(Q_PART)
                    stack, part = ((qs, Q_PART[n]), (ks, K_PART[n]))[which]
                    src = parts_d[which, bass.ds(unit, 1), :, :, part, :].rearrange("u s g t -> (u s g) t")
                    sp.dma_start(stack[n * HD:(n + 1) * HD, slot].rearrange("r s h t -> r (s h) t"),
                                 src.rearrange("(g r) t -> r g t", r=HD)).then_inc(stack_in[slot], 16)

            def load_max_rows(items, slot, half):
                sp.wait_ge(ring_free, items)
                sp.dma_start(qs[SROWS:MROWS, slot, half].rearrange("p h (t q) -> p (h t) q", q=P), mt[:, half, :]
                             ).then_inc(mrow_in[half], 16)

            for k in range(2 * NC + 2):
                send_parts(k)
            for n in range(QBUF):
                sp.wait_ge(part_out[n], sent(2 * NC, n))
            sp.wait_ge(wsplit_lo, 2)
            sp.wait_ge(w2_lo, NH // 2)
            sp.wait_ge(w13_lo, 2 * WSPLIT)
            for k in range(2 * NC + 2, 4 * NC):
                n = k - (2 * NC + 2)
                load_stack(0, 0, range(STACK_LOADS)[4 * n:4 * n + 4])
                send_parts(k)
            load_stack(1, 1)
            for n in range(QBUF):
                sp.wait_ge(part_out[n], sent(4 * NC, n))
            for half in range(2):
                load_max_rows(FIRST_ITEMS.index(("mt", half, 0, 0)) + 1, 0, half)

            def body(unit, par, more):
                load_max_rows(ring_count(unit, ("mt", 0, 0, 0)), 1 - par, 0)
                if more:
                    sp.wait_ge(s_ps, (unit + 1) * (2 * NSTEP))
                    load_stack(unit + 2, par)
                load_max_rows(ring_count(unit, ("mt", 1, 0, 0)), 1 - par, 1)

            with sp.Fori(0, UNITS // 2 - 1) as it:
                body(it * 2, 0, True)
                body(it * 2 + 1, 1, True)
            body(UNITS - 2, 0, False)

            for c in range(NC):
                sp.wait_ge(res_added, RES["FF2"] + c + 1)
                sp.dma_start(chunk_of(out_d.rearrange("(t p) n -> p t n", p=P), c), chunk_of(x, c)
                             ).then_inc(out_sent, 16)
            sp.wait_ge(out_sent, 16 * NC)

        @block.tensor
        def _(pe):
            PASSES = ((0, 0), (0, 1), (1, 0))

            def transposes(place, src, done):
                for d in range(ND):
                    for t in range(TPC):
                        last = nc.tensor.transpose(place[d][:, t * P:(t + 1) * P], src(t, d), ident[:])
                last.then_inc(done, 1)

            def norm_transposes(kind, c, place=T_BANKS):
                n = fill_no(kind, c)
                pe.wait_ge(xn_done, n + 1)
                if place is T_BANKS and (not isinstance(n, int) or n > 0):
                    pe.wait_ge(xt_hi, n)
                    pe.wait_ge(xt_lo, n)
                transposes(place, lambda t, d: xn[:, t, d * P:(d + 1) * P], xt_ps)

            def att_transposes(c):
                if isinstance(c, int) and c == 0:
                    pe.wait_ge(o_done, GROUPS * 2)
                    transposes(FREE_BANKS, lambda t, d: o_tok[:, t, 2 * d:2 * d + 2, :].rearrange("p g n -> p (g n)"), at_ps)
                else:
                    pe.wait_ge(o_taken, c)
                    pe.wait_ge(xt_hi, fill_no("OUT", c))
                    pe.wait_ge(xt_lo, fill_no("OUT", c))
                    transposes(T_BANKS, lambda t, d: o_now[:, t, d * P:(d + 1) * P], at_ps)

            def output_projection(c, place=T_BANKS):
                pe.wait_ge(at_lo, c + 1)
                pe.wait_ge(at_hi, c + 1)
                for t in range(TPC):
                    for n, (d, (wp, xp)) in enumerate([(d, p) for d in range(ND) for p in PASSES]):
                        last = nc.tensor.matmul(place[t // 2][:, (t % 2) * D:(t % 2 + 1) * D],
                                                xa[:, xp, d, t * P:(t + 1) * P], wo[:, wp, d, :],
                                                start=n == 0 and t % 2 == 0, stop=n == 5, skip_group_check=True)
                last.then_inc(wo_done, 1)

            def up(k, c, hc):
                for ps, w, freed, done in ((ps_gate, w1, silu_done, gate_done), (ps_lin, w3, u_done, lin_done)):
                    if not isinstance(k, int) or k >= 2:
                        pe.wait_ge(freed, k - 1)
                    n = 0
                    for d in range(ND):
                        for wp, xp in PASSES:
                            last = nc.tensor.matmul(ps[hc % 2][:], w[:, wp, d, hc * P:(hc + 1) * P],
                                                    xt[:, bass.ds(c, 1), xp, d, :].rearrange("p o t -> p (o t)"),
                                                    start=n == 0, stop=n == 5)
                            n += 1
                    last.then_inc(done, 1)

            def down(k, hc, chunks_before):
                pe.wait_ge(ul_done, k + 1)
                if hc == 0 and (not isinstance(chunks_before, int) or chunks_before > 0):
                    pe.wait_ge(res_added, chunks_before)
                for t in range(TPC):
                    for n, (wp, up_) in enumerate(PASSES):
                        lhs = (uh, ul)[up_]
                        last = nc.tensor.matmul(ps_down[:, t // 2, (t % 2) * D:(t % 2 + 1) * D],
                                                lhs[:, hc % 2, t * P:(t + 1) * P], w2[:, wp, hc, :],
                                                start=hc == 0 and n == 0 and t % 2 == 0,
                                                stop=hc == NH - 1 and n == 2, skip_group_check=True)
                last.then_inc(down_done if hc == NH - 1 else down_used, 1)

            def feed_forward(layer, fills, c, before, extra):
                k0 = (layer * NC + c) * NH
                res = (RES["FF"], RES["FF2"])[layer] + c
                pe.wait_ge(xt_lo, fills)
                pe.wait_ge(xt_hi, fills)
                for hc in range(NH):
                    up(k0 + hc, c, hc)
                    if hc == 0:
                        before()
                    else:
                        down(k0 + hc - 1, hc - 1, res)
                    extra(hc)

            def last_down(layer, c):
                down((layer * NC + c) * NH + NH - 1, NH - 1, 0)

            pe.wait_ge(ld_ident, 16)
            norm_transposes("IN", 0)

            def hadamard(i):
                if i == 0:
                    pe.wait_ge(ld_had, 16)
                    pe.wait_ge(fly_sum, 3)
                    pe.wait_ge(fly_diff, 3)
                if i >= 2:
                    pe.wait_ge(w2_lo, i - 1)
                nc.tensor.matmul(ps_down[:, i % 2, :], had[:], fly_out(i),
                                 start=True, stop=True).then_inc(had_ps, 1)

            def first_extra(hc):
                if hc < 2:
                    hadamard(2 * hc)
                    hadamard(2 * hc + 1)
                if hc == 1:
                    pe.wait_ge(w2_lo, NH // 2)
                    pe.wait_ge(w2_hi, NH // 2)
                if hc in (2, 4, 6):
                    norm_transposes("IN", hc // 2)

            pe.wait_ge(xt_lo, 1)
            pe.wait_ge(xt_hi, 1)
            for hc in range(NH):
                if hc % 2 == 0:
                    pe.wait_ge(w13_lo, hc + 2)
                    pe.wait_ge(w13_hi, hc + 2)
                up(hc, 0, hc)
                first_extra(hc)
                if hc >= 1:
                    down(hc - 1, hc - 1, 0)

            with pe.Fori(1, NC) as c:
                feed_forward(0, fill_no("IN", c) + 1, c, lambda: last_down(0, c - 1),
                             lambda hc: norm_transposes("FF", c - 1) if hc == 3 else None)
            last_down(0, NC - 1)

            pe.wait_ge(silu_done, NC * NH)
            pe.wait_ge(u_done, NC * NH)
            pe.wait_ge(wsplit_lo, 2)
            for c in range(NC):
                pe.wait_ge(xt_lo, fill_no("FF", c) + 1)
                pe.wait_ge(xt_hi, fill_no("FF", c) + 1)
                for ct in range(4):
                    k = 4 * c + ct
                    if k >= 2:
                        pe.wait_ge(qf_done, k - 1)
                    for n, (d, (wp, xp)) in enumerate([(d, p) for d in range(ND) for p in PASSES]):
                        last = nc.tensor.matmul(banks[k % 2][:], wqkv[:, wp, d, ct * P:(ct + 1) * P],
                                                xt[:, c, xp, d, :], start=n == 0, stop=n == 5)
                    last.then_inc(qk_ps, 1)
                for vv in range(2):
                    i = 2 * c + vv
                    if i >= 2:
                        pe.wait_ge(v_done, i - 1)
                    for tt in range(2):
                        t = 2 * vv + tt
                        for n, (d, (wp, xp)) in enumerate([(d, p) for d in range(ND) for p in PASSES]):
                            last = nc.tensor.matmul(banks[2 + i % 2][:, tt * D:(tt + 1) * D],
                                                    xt[:, c, xp, d, t * P:(t + 1) * P], wqkv[:, wp, d, 2 * D:3 * D],
                                                    start=tt == 0 and n == 0, stop=n == 5, skip_group_check=True)
                    last.then_inc(v_ps, 1)
                if c == 0:
                    norm_transposes("FF", NC - 1)

            def suffix_sums(i):
                if i < KT - 2:
                    pe.wait_ge(suf_done, KT - 2 - i)
                    pe.wait_ge(wsum_done, KT - 2 - i)
                rest = {KT - 1: None, KT - 2: v_all[:, KT - 1]}.get(i, w_sum(i))
                out = ps_down[:, i % 2, :].rearrange("p (u n) -> p u n", u=UNITS)
                last = nc.tensor.matmul(out, after[:], v_all[:, i], start=True, stop=rest is None)
                if rest is not None:
                    last = nc.tensor.matmul(out, ones[:], rest, start=False, stop=True)
                last.then_inc(suf_ps, 1)

            def ring_item(item, bank, free_at, unit, par, prev_unit):
                kind, a, h, piece = item
                out = ps_ring[bank]
                if free_at is not None:
                    pe.wait_ge(ring_free, free_at)
                if kind == "red":
                    n = red_width(a, piece)
                    diagonal = piece == a // TPC
                    last = nc.tensor.matmul(out[:, 0:n], qs[0:SROWS, par, a // TPC, h, (a % TPC) * P:(a % TPC + 1) * P],
                                            ks[0:SROWS, par, piece, h, 0:n], start=True, stop=not diagonal)
                    if diagonal:
                        last = nc.tensor.matmul(out[:, n - P:n], ident_b[:], tri_b[:], start=False, stop=True)
                elif kind == "mt":
                    loop_wait(pe, mp_cut, unit * 2 + a + 1)
                    last = nc.tensor.transpose(out[0:PARTS * MT, 0:P // 2].bitcast(BF16),
                                               mpart[:, a].rearrange("p c h t -> p (c h t)"), ident_b[:])
                else:
                    pe.wait_ge(o_copied, prev_unit * 2 + a + 1)
                    for t in range(TPC):
                        last = nc.tensor.transpose(out[:, t * P:(t + 1) * P], o_raw[:, t * P:(t + 1) * P], ident[:])
                last.then_inc(ring_full, 1)

            def scores(step, s, p, par, unit):
                c, j, q0 = STEPS[s]
                if p == 0 and s in (0, STEPS_C0):
                    pe.wait_ge(mrow_in[c], (unit + 1) * 16)
                if not isinstance(step, int) or step > 0:
                    pe.wait_ge(p_done, step * 2 - 1 + p)
                for hh in range(2):
                    h = 2 * p + hh
                    last = nc.tensor.matmul(ps_s[p][:, hh, 0:CH - q0], ks[:, par, j // TPC, h, (j % TPC) * P:(j % TPC + 1) * P],
                                            qs[:, par, c, h, q0:CH], start=True, stop=True)
                last.then_inc(s_ps, 1)

            def values(step, s, par, unit):
                c, j, q0 = STEPS[s]
                pe.wait_ge(p_done, step * 2 + 2)
                if s in DIAG:
                    pe.wait_ge(p_masked, unit * len(DIAG) + (DIAG.index(s) + 1))
                if s == 0:
                    pe.wait_ge(vg_done, unit + 1)
                if s in (0, STEPS_C0) and (not isinstance(unit, int) or unit * 2 + c > 0):
                    pe.wait_ge(o_copied, unit * 2 + c)
                for h in range(GH):
                    last = nc.tensor.matmul(ps_o[VW * h:VW * (h + 1), q0:CH], vg[:, par, j, h, :],
                                            probs[:, s % RING, h, 0:CH - q0], start=j == 0,
                                            stop=j * P == (c + 1) * CH - P, tile_position=(0, VW * h),
                                            skip_group_check=True)
                last.then_inc(pv_done, 1)

            def first_scores(s):
                for p in range(2):
                    scores(s, s, p, 0, 0)
                if s > 0:
                    values(s - 1, s - 1, 0, 0)

            pe.wait_ge(qf_done, 4 * NC)
            pe.wait_ge(v_done, 2 * NC)
            pe.wait_ge(stack_ones, 1)
            pe.wait_ge(stack_in[0], 16 * STACK_LOADS)
            for n, item in enumerate(FIRST_ITEMS):
                if n == FIRST_SCORES:
                    pe.wait_ge(suf_done, KT)
                if n >= FIRST_SCORES and (n - FIRST_SCORES) % FIRST_GAP == 0 and (n - FIRST_SCORES) // FIRST_GAP < AHEAD:
                    first_scores((n - FIRST_SCORES) // FIRST_GAP)
                ring_item(item, (n + 2) % RING, n - 2 if n >= RING else None, 0, 0, None)
                if n % 2 == 1 and SUFFIX_FROM <= n < SUFFIX_FROM + 2 * KT:
                    suffix_sums(KT - 1 - (n - SUFFIX_FROM) // 2)

            def body(unit, par, visit, last):
                ring0 = NFIRST + unit * NBODY
                pos = 0
                if not last:
                    pe.wait_ge(stack_in[1 - par], visit * (16 * STACK_LOADS))
                for t in range(NSTEP if not last else NSTEP - AHEAD):
                    s = (AHEAD + t) % NSTEP
                    step = unit * NSTEP + (AHEAD + t)
                    here = t < NSTEP - AHEAD
                    items = BODY[t] if not last else [i for i in BODY[t] if i[0] == "ot"]
                    if last and t == AT_SLOT:
                        pe.wait_ge(ring_free, ring0)
                        att_transposes(0)
                    if last and t == WO_SLOT:
                        output_projection(0, FREE_BANKS)
                    if last and t == OUT_SLOT:
                        norm_transposes("OUT", 0, FREE_BANKS)
                    for p in range(2):
                        scores(step, s, p, par if here else 1 - par, unit if here else unit + 1)
                        for item in items[p * len(items) // 2:(p + 1) * len(items) // 2]:
                            if last:
                                free_at = ring0 + pos
                            else:
                                free_at = ring0 + (pos - 2 if pos >= RING else (0, -2, -1)[pos])
                            ring_item(item, pos % RING if not last else 0, free_at, unit + 1, 1 - par, unit)
                            pos += 1
                    was_here = t - 1 < NSTEP - AHEAD
                    values(step - 1, (s - 1) % NSTEP, par if was_here else 1 - par, unit if was_here else unit + 1)
                if last:
                    values(UNITS * NSTEP - 1, NSTEP - 1, par, unit)
                    ring_item(("ot", 1, 0, 0), 0, ring0 + pos, unit, par, unit)

            with pe.Fori(0, UNITS // 2 - 1) as it:
                body(it * 2, 0, it + 1, False)
                body(it * 2 + 1, 1, it + 2, False)
            body(UNITS - 2, 0, UNITS // 2, False)
            body(UNITS - 1, 1, None, True)

            pe.wait_ge(ring_free, RING_TOTAL)
            pe.wait_ge(p_done, 2 * NSTEP * UNITS)
            pe.wait_ge(o_copied, 2 * UNITS)

            def following(c):
                def extra(hc):
                    if hc == 0:
                        att_transposes(c)
                    if hc == 2:
                        output_projection(c)
                    if hc == 5:
                        norm_transposes("OUT", c)
                return extra

            feed_forward(1, fill_no("OUT", 0) + 1, 0, lambda: None, following(1))
            with pe.Fori(1, NC - 1) as c:
                feed_forward(1, fill_no("OUT", c) + 1, c, lambda: last_down(1, c - 1), following(c + 1))
            feed_forward(1, fill_no("OUT", NC - 1) + 1, NC - 1, lambda: last_down(1, NC - 2), lambda hc: None)
            last_down(1, NC - 1)

        @block.scalar
        def _(act):
            def at_fill_hi(c):
                act.wait_ge(at_ps, c + 1)
                for d in range(ND):
                    last = nc.scalar.copy(xa[:, 0, d, :], ps_t[:, d, :])
                last.then_inc(at_hi, 1)

            def fill_hi(kind, c):
                act.wait_ge(xt_ps, fill_no(kind, c) + 1)
                for d in range(ND):
                    last = nc.scalar.copy(xt[:, bass.ds(c, 1), 0, d, :].rearrange("p o t -> p (o t)"), ps_t[:, d, :])
                last.then_inc(xt_hi, 1)

            def w13_part(n):
                w, raw, loaded = ((w1, w1_raw, ld_w1), (w3, w3_raw, ld_w3))[n % 2]
                act.wait_ge(loaded[n // WSPLIT], 16)
                cols = slice((n // 2) * WP, (n // 2 + 1) * WP)
                nc.scalar.copy(w[:, 0, :, cols], raw[:, :, cols]).then_inc(w13_hi, 1)

            def gate(k, hc):
                act.wait_ge(gate_done, k + 1)
                if not isinstance(k, int) or k >= 2:
                    act.wait_ge(ul_done, k - 1)
                nc.scalar.activation(u[:, hc % 2, :], ps_gate[hc % 2][:], ACT.Silu).then_inc(silu_done, 1)

            def hidden_hi(k, hc, downs):
                act.wait_ge(u_done, k + 1)
                if downs is not None:
                    downs()
                nc.scalar.copy(uh[:, hc % 2, :], u[:, hc % 2, :]).then_inc(uh_done, 1)

            def downs_before(eng, layer, c, hc):
                if hc >= 2:
                    eng.wait_ge(down_used, (layer * NC + c) * (NH - 1) + hc - 1)
                elif isinstance(c, int) and c == 0 and layer == 0:
                    return
                elif hc == 0:
                    eng.wait_ge(down_used, (layer * NC + c) * (NH - 1))
                else:
                    eng.wait_ge(down_done, c + (RES["FF"], RES["FF2"])[layer])

            def feed_forward(layer, c, extra):
                for hc in range(NH):
                    k = (layer * NC + c) * NH + hc
                    gate(k, hc)
                    hidden_hi(k, hc, lambda: downs_before(act, layer, c, hc))
                    extra(hc)

            def w2_part(i):
                act.wait_ge(had_ps, i + 1)
                nc.scalar.activation(w2[:, 0, 2 * i:2 * i + 2, :], ps_down[:, i % 2, :].rearrange("p (a n) -> p a n", a=2),
                                     ACT.Copy, scale=W2_SCALE).then_inc(w2_hi, 1)

            w13_part(0)
            w13_part(1)
            fill_hi("IN", 0)
            for hc in range(NH):
                gate(hc, hc)
                if hc < 2:
                    w2_part(2 * hc)
                    w2_part(2 * hc + 1)
                hidden_hi(hc, hc, lambda: downs_before(act, 0, 0, hc))
                if hc < 3:
                    w13_part(2 * hc + 2)
                    w13_part(2 * hc + 3)
                if hc in (2, 4, 6):
                    fill_hi("IN", hc // 2)

            with act.Fori(1, NC) as c:
                feed_forward(0, c, lambda hc: fill_hi("FF", c - 1) if hc == 3 else None)

            act.wait_ge(ld_const, 16 * 7)
            def middle_part(k):
                act.wait_ge(r1_done, k + 1)
                nc.scalar.copy(stage[:, k % QBUF, 1, :], r1[:, k % 2, :]).then_inc(qm_done, 1)

            for k in range(4 * NC):
                if k == LAST_FILL:
                    fill_hi("FF", NC - 1)
                act.wait_ge(qk_ps, k + 1)
                if k >= 2:
                    act.wait_ge(r1_done, k - 1)
                nc.scalar.activation(qf[:, k % 2, :], banks[k % 2][:], ACT.Identity,
                                     bias=bqk[:, k % 4:k % 4 + 1]).then_inc(qf_done, 1)
                act.wait_ge(qf_done, k + 1)
                if k >= QBUF:
                    act.wait_ge(part_out[k % QBUF], sent(k - QBUF + 1, k % QBUF))
                nc.scalar.copy(stage[:, k % QBUF, 0, :], qf[:, k % 2, :]).then_inc(qh_done, 1)
                if k >= 1:
                    middle_part(k - 1)
            middle_part(4 * NC - 1)

            act.wait_ge(ql_done, 4 * NC)
            for n in range(QBUF):
                act.wait_ge(part_out[n], sent(4 * NC, n))
            for n in range(KT):
                act.wait_ge(suf_ps, n + 1)
                i = KT - 1 - n
                nc.scalar.copy(suffix[:, i], ps_down[:, i % 2, :].rearrange("p (u n) -> p u n", u=UNITS)
                               ).then_inc(suf_done, 1)

            def exponentials(step, s, p):
                c, j, q0 = STEPS[s]
                act.wait_ge(s_ps, step * 2 + p + 1)
                if p == 0 and (not isinstance(step, int) or step >= RING):
                    act.wait_ge(pv_done, step - (RING - 1))
                nc.scalar.activation(probs[:, s % RING, 2 * p:2 * p + 2, 0:CH - q0], ps_s[p][:, :, 0:CH - q0],
                                     ACT.Exp, scale=SCALE).then_inc(p_done, 1)

            def copy_o(unit, c):
                act.wait_ge(pv_done, unit * NSTEP + (STEPS_C0, NSTEP)[c])
                if c == 1:
                    act.wait_ge(ring_full, ring_count(unit, ("ot", 0, 0, 0)))
                elif not isinstance(unit, int) or unit > 0:
                    act.wait_ge(ring_full, (unit - 1) * NBODY + (NFIRST + BODY_ITEMS.index(("ot", 1, 0, 0)) + 1))
                nc.scalar.copy(o_raw[:], ps_o[:]).then_inc(o_copied, 1)

            for s in range(AHEAD):
                for p in range(2):
                    exponentials(s, s, p)

            def body(unit, par, last):
                for t in range(NSTEP if not last else NSTEP - AHEAD):
                    if t == 1:
                        act.wait_ge(ea_done, unit + 1)
                        nc.scalar.activation(et[:, par], ea[:], ACT.Exp).then_inc(et_done, 1)
                    for p in range(2):
                        exponentials(unit * NSTEP + (AHEAD + t), (AHEAD + t) % NSTEP, p)
                        if p == 0 and t == STEPS_C0 - AHEAD + 1:
                            copy_o(unit, 0)
                        if p == 0 and t == NSTEP - AHEAD + 1:
                            copy_o(unit, 1)
                if last:
                    copy_o(unit, 1)

            with act.Fori(0, UNITS // 2 - 1) as it:
                body(it * 2, 0, False)
                body(it * 2 + 1, 1, False)
            body(UNITS - 2, 0, False)
            body(UNITS - 1, 1, True)

            def following(c):
                def extra(hc):
                    if hc == 0:
                        at_fill_hi(c)
                    if hc == 5:
                        fill_hi("OUT", c)
                return extra

            feed_forward(1, 0, following(1))
            with act.Fori(1, NC - 1) as c:
                feed_forward(1, c, following(c + 1))
            feed_forward(1, NC - 1, lambda hc: None)

        @block.vector
        def _(dve):
            def statistics(kind, c):
                n = fill_no(kind, c)
                if not isinstance(n, int) or n > 0:
                    loop_wait(dve, rstd_done, n)
                for t in range(TPC):
                    last = nc.vector.bn_stats(bn[:, t, :], x[:, bass.ds(c * TPC + t, 1), :].rearrange("p o n -> p (o n)"))
                last.then_inc(bn_done, 1)
                loop_wait(dve, bn_done, n + 1)
                for t in range(TPC):
                    last = nc.vector.bn_aggr(mv[:, t, :], bn[:, t, :])
                last.then_inc(mv_done, 1)

            def normalise(kind, c):
                n = fill_no(kind, c)
                dve.wait_ge(rstd_done, n + 1)
                if not isinstance(n, int) or n > 0:
                    dve.wait_ge(xt_ps, fill_no(kind, c))
                for t in range(TPC):
                    last = nc.vector.tensor_scalar(xn[:, t, :], x[:, bass.ds(c * TPC + t, 1), :].rearrange("p o n -> p (o n)"),
                                                   mv[:, t, 0:1], rstd[:, t:t + 1], ALU.subtract, ALU.mult)
                last.then_inc(xn_done, 1)

            def fill_lo(kind, c):
                dve.wait_ge(xt_hi, fill_no(kind, c) + 1)
                for d in range(ND):
                    view = [xt[:, bass.ds(c, 1), part, d, :].rearrange("p o t -> p (o t)") for part in range(2)]
                    last = nc.vector.tensor_tensor(view[1], ps_t[:, d, :], view[0].bitcast(F32), ALU.subtract)
                last.then_inc(xt_lo, 1)

            def add_attention(c, place=T_BANKS):
                dve.wait_ge(wo_done, c + 1)
                for i in range(2):
                    xc = x[:, bass.ds(c * TPC + 2 * i, 2), :]
                    last = nc.vector.tensor_tensor(xc, xc, place[i].rearrange("p (a n) -> p a n", a=2), ALU.add)
                last.then_inc(att_added, 1)

            def at_fill_lo(c):
                dve.wait_ge(at_hi, c + 1)
                for d in range(ND):
                    last = nc.vector.tensor_tensor(xa[:, 1, d, :], ps_t[:, d, :], xa[:, 0, d, :].bitcast(F32), ALU.subtract)
                last.then_inc(at_lo, 1)

            def fill_both(ready, n, dst, hi_done, lo_done):
                dve.wait_ge(ready, n)
                for d in range(ND):
                    last = nc.vector.tensor_copy(dst(0, d), FREE_BANKS[d])
                last.then_inc(hi_done, 1)
                dve.wait_ge(hi_done, n)
                for d in range(ND):
                    last = nc.vector.tensor_tensor(dst(1, d), FREE_BANKS[d], dst(0, d).bitcast(F32), ALU.subtract)
                last.then_inc(lo_done, 1)

            def add_residual(phase, c):
                dve.wait_ge(down_done, RES[phase] + c + 1)
                for i in range(2):
                    xc = x[:, bass.ds(c * TPC + 2 * i, 2), :]
                    last = nc.vector.tensor_tensor(xc, xc, ps_down[:, i, :].rearrange("p (a n) -> p a n", a=2), ALU.add)
                last.then_inc(res_added, 1)

            def butterflies(stage_no):
                if stage_no:
                    dve.wait_ge(fly_diff, stage_no)
                    dve.wait_ge(fly_sum, stage_no)
                else:
                    dve.wait_ge(ld_w2, 16)
                a, b, s_, _ = fly_views(stage_no)
                nc.vector.tensor_tensor(s_, a, b, ALU.add).then_inc(fly_sum, 1)

            def w13_part(n):
                w, raw = ((w1, w1_raw), (w3, w3_raw))[n % 2]
                dve.wait_ge(w13_hi, n + 1)
                cols = slice((n // 2) * WP, (n // 2 + 1) * WP)
                nc.vector.tensor_tensor(w[:, 1, :, cols], raw[:, :, cols], w[:, 0, :, cols].bitcast(F32),
                                        ALU.subtract).then_inc(w13_lo, 1)

            def product(k, hc):
                dve.wait_ge(silu_done, k + 1)
                dve.wait_ge(lin_done, k + 1)
                nc.vector.tensor_tensor(u[:, hc % 2, :], u[:, hc % 2, :], ps_lin[hc % 2][:], ALU.mult
                                        ).then_inc(u_done, 1)

            def hidden_lo(k, hc):
                dve.wait_ge(uh_done, k + 1)
                nc.vector.tensor_tensor(ul[:, hc % 2, :], u[:, hc % 2, :], uh[:, hc % 2, :].bitcast(F32),
                                        ALU.subtract).then_inc(ul_done, 1)

            def w2_part(i):
                dve.wait_ge(w2_hi, i + 1)
                nc.vector.scalar_tensor_tensor(
                    w2[:, 1, 2 * i:2 * i + 2, :], ps_down[:, i % 2, :].rearrange("p (a n) -> p a n", a=2), W2_SCALE,
                    w2[:, 0, 2 * i:2 * i + 2, :].bitcast(F32), ALU.mult, ALU.subtract).then_inc(w2_lo, 1)

            dve.wait_ge(ld_x[0], 16)
            statistics("IN", 0)
            butterflies(0)
            normalise("IN", 0)
            w13_part(0)
            w13_part(1)
            butterflies(1)
            fill_lo("IN", 0)
            butterflies(2)
            for hc in range(NH):
                if hc in (0, 2, 4):
                    dve.wait_ge(ld_x[hc // 2 + 1], 16)
                    statistics("IN", hc // 2 + 1)
                product(hc, hc)
                if hc < 2:
                    w2_part(2 * hc)
                    w2_part(2 * hc + 1)
                hidden_lo(hc, hc)
                if hc < 3:
                    w13_part(2 * hc + 2)
                    w13_part(2 * hc + 3)
                if hc in (1, 3, 5):
                    normalise("IN", (hc + 1) // 2)
                if hc in (2, 4, 6):
                    fill_lo("IN", hc // 2)
            dve.wait_ge(ld_const, 16 * 7)
            nc.vector.tensor_copy(ident_b[:], ident[:]).then_inc(const_cut, 1)
            nc.vector.tensor_copy(tri_b[:], tri_f[:]).then_inc(const_cut, 1)

            def feed_forward(layer, c, extra):
                for hc in range(NH):
                    k = (layer * NC + c) * NH + hc
                    product(k, hc)
                    hidden_lo(k, hc)
                    extra(hc)

            def tail(phase, norm, c):
                def extra(hc):
                    if hc == 0:
                        add_residual(phase, c)
                    if norm and hc == 1:
                        dve.wait_ge(res_added, RES[phase] + c + 1)
                        statistics(norm, c)
                    if norm and hc == 2:
                        normalise(norm, c)
                    if norm and hc == 3:
                        fill_lo(norm, c)
                return extra

            with dve.Fori(1, NC) as c:
                feed_forward(0, c, tail("FF", "FF", c - 1))

            def values_in(i):
                dve.wait_ge(v_ps, i + 1)
                b, j = i // 4, 2 * (i % 4)
                for tt in range(2):
                    last = nc.vector.tensor_tensor(
                        v_all[:, j + tt, b * GROUPS:(b + 1) * GROUPS, :],
                        banks[2 + i % 2][:, tt * D:(tt + 1) * D].rearrange("p (g n) -> p g n", g=GROUPS),
                        bv[:].rearrange("p (g n) -> p g n", g=GROUPS), ALU.add)
                last.then_inc(v_done, 1)

            def last_part(k):
                dve.wait_ge(qm_done, k + 1)
                nc.vector.tensor_tensor(stage[:, k % QBUF, 2, :], r1[:, k % 2, :], stage[:, k % QBUF, 1, :],
                                        ALU.subtract).then_inc(ql_done, 1)

            end = tail("FF", "FF", NC - 1)
            end(0)
            for k in range(4 * NC):
                dve.wait_ge(qh_done, k + 1)
                if k >= 2:
                    dve.wait_ge(qm_done, k - 1)
                    dve.wait_ge(ql_done, k - 1)
                nc.vector.tensor_tensor(r1[:, k % 2, :], qf[:, k % 2, :], stage[:, k % QBUF, 0, :], ALU.subtract
                                        ).then_inc(r1_done, 1)
                if k >= 1:
                    last_part(k - 1)
                if k < 2:
                    end(k + 1)
                if k == LAST_FILL - 1:
                    end(3)
                if k % 4 == 3:
                    values_in(2 * (k // 4))
                    values_in(2 * (k // 4) + 1)
            last_part(4 * NC - 1)

            def ring_item(item, bank, after_count, unit, par, prev_unit, prev_par):
                kind, a, h, piece = item
                dve.wait_ge(ring_full, after_count)
                src = ps_ring[bank]
                if kind == "red":
                    at = RED_A.index(item) if a < TPC else NA + RED_B.index(item)
                    nc.vector.reduce_max(mp[:, at:at + 1], src[:, 0:red_width(a, piece)], AX.X).then_inc(ring_free, 1)
                    if item == RED_B[-1]:
                        dve.wait_ge(ring_free, after_count)
                        two = mp[:, NA:NA + NB].rearrange("p (i c h) -> p c h i", c=2, h=GH)
                        nc.vector.tensor_tensor(mb[:], two[:, 0], two[:, 1], ALU.max).then_inc(mb_done, 1)
                        dve.wait_ge(mb_done, unit + 1)
                        nc.vector.scalar_tensor_tensor(mneg[:, par, :, TPC:KT], mb[:], -1.0, neg_floor[:],
                                                       ALU.mult, ALU.min).then_inc(mneg_done, 1)
                elif kind == "mt":
                    if not isinstance(unit, int) or unit > 0:
                        dve.wait_ge(mrow_in[a], unit * 16)
                    nc.vector.tensor_copy(mt[:, a, :], src[0:PARTS * MT, 0:P // 2].bitcast(BF16)).then_inc(ring_free, 1)
                else:
                    oc = prev_unit * 2 + a
                    cols = slice(a * TPC, (a + 1) * TPC)
                    four = src[:].rearrange("p (t h n) -> p t h n", t=TPC, h=GH)
                    dve.wait_ge(em_done, prev_unit + 1)
                    dve.wait_ge(o_done, oc + 1)
                    nc.vector.tensor_tensor(dsum[:], four[:, :, :, HD], ecnt[:, prev_par, :, cols].rearrange("p h t -> p t h"),
                                            ALU.add).then_inc(dsum_done, 1)
                    nc.vector.tensor_tensor(num[:], four[:, :, :, 0:HD], em[:, prev_par, cols], ALU.add
                                            ).then_inc(ring_free, 1)
                    dve.wait_ge(dsum_done, oc + 1)
                    nc.vector.reciprocal(rcp[:], dsum[:]).then_inc(rcp_done, 1)

            for n, item in enumerate(FIRST_ITEMS):
                ring_item(item, (n + 2) % RING, n + 1, 0, 0, None, None)

            def body(unit, par, last):
                ring0 = NFIRST + unit * NBODY
                items = BODY_ITEMS if not last else LAST_ITEMS
                if last:
                    fill_both(at_ps, 1, lambda part, d: xa[:, part, d, :], at_hi, at_lo)
                    dve.wait_ge(bo_added, 1)
                    add_attention(0, FREE_BANKS)
                    dve.wait_ge(att_added, 1)
                    statistics("OUT", 0)
                for n, item in enumerate(items):
                    ring_item(item, n % RING if not last else 0, ring0 + n + 1, unit + 1, 1 - par, unit, par)
                    if last and n == 0:
                        normalise("OUT", 0)
                        fill_both(xt_ps, fill_no("OUT", 0) + 1, lambda part, d: xt[:, 0, part, d, :], xt_hi, xt_lo)

            with dve.Fori(0, UNITS // 2 - 1) as it:
                body(it * 2, 0, False)
                body(it * 2 + 1, 1, False)
            body(UNITS - 2, 0, False)
            body(UNITS - 1, 1, True)

            dve.wait_ge(o_done, UNITS * 2 + 1)

            def following(before, c):
                def extra(hc):
                    if hc == 0:
                        if before is not None:
                            add_residual("FF2", before)
                        if c is not None:
                            at_fill_lo(c)
                    if c is not None and hc == 3:
                        add_attention(c)
                        dve.wait_ge(att_added, c + 1)
                        statistics("OUT", c)
                    if c is not None and hc == 4:
                        normalise("OUT", c)
                    if c is not None and hc == 5:
                        fill_lo("OUT", c)
                return extra

            feed_forward(1, 0, following(None, 1))
            with dve.Fori(1, NC - 1) as c:
                feed_forward(1, c, following(c - 1, c + 1))
            feed_forward(1, NC - 1, following(NC - 2, None))
            add_residual("FF2", NC - 1)

        @block.gpsimd
        def _(pool):
            nc.gpsimd.memset(neg_half[:], -0.5).then_inc(pool_const, 1)
            nc.gpsimd.memset(ones[:], 1.0).then_inc(pool_const, 1)

            def inverse_deviation(kind, c):
                n = fill_no(kind, c)
                loop_wait(pool, mv_done, n + 1)
                if not isinstance(n, int) or n > 0:
                    loop_wait(pool, xn_done, n)
                nc.gpsimd.tensor_scalar_add(ve[:], mv[:, :, 1], EPS).then_inc(ve_done, 1)
                loop_wait(pool, ve_done, n + 1)
                nc.gpsimd.tensor_tensor(rstd[:], ve[:], neg_half[:], ALU.pow).then_inc(rstd_done, 1)

            pool.wait_ge(pool_const, 2)
            inverse_deviation("IN", 0)
            for stage_no in range(3):
                if stage_no:
                    pool.wait_ge(fly_sum, stage_no)
                    pool.wait_ge(fly_diff, stage_no)
                else:
                    pool.wait_ge(ld_w2, 16)
                a, b, _, d_ = fly_views(stage_no)
                nc.gpsimd.tensor_tensor(d_, a, b, ALU.subtract).then_inc(fly_diff, 1)
            for c in range(1, NC):
                inverse_deviation("IN", c)
            for n, (w, raw, loaded) in enumerate(((wqkv, wqkv_raw, ld_wqkv), (wo, wo_raw, ld_wo))):
                pool.wait_ge(loaded, 16)
                nc.gpsimd.tensor_copy(w[:, 0], raw[:]).then_inc(wsplit_hi, 1)
                pool.wait_ge(wsplit_hi, n + 1)
                nc.gpsimd.tensor_tensor(w[:, 1], raw[:], w[:, 0].bitcast(F32), ALU.subtract).then_inc(wsplit_lo, 1)
                pool.wait_ge(wsplit_lo, n + 1)
            with pool.Fori(1, NC) as c:
                inverse_deviation("FF", c - 1)
            pool.wait_ge(w13_lo, 2 * WSPLIT)
            pool.wait_ge(w2_lo, NH // 2)
            pool.wait_ge(rstd_done, 2 * NC - 1)
            nc.gpsimd.memset(ks[SROWS:MROWS], 1.0).then_inc(stack_ones, 1)
            pool.wait_ge(stack_ones, 1)
            inverse_deviation("FF", NC - 1)
            pool.wait_ge(ld_const, 16 * 7)
            for c in range(NC):
                pool.wait_ge(xn_done, fill_no("FF", c) + 1)
                last = nc.gpsimd.tensor_tensor(chunk_of(x, c), chunk_of(x, c), bo[:].unsqueeze(1).broadcast_to([P, TPC, D]),
                                               ALU.add)
            last.then_inc(bo_added, 1)

            pool.wait_ge(down_done, NC)
            nc.gpsimd.memset(vg[:], 1.0).then_inc(vg_ones, 1)
            nc.gpsimd.memset(num[:], 0.0).then_inc(o_done, 1)
            pool.wait_ge(v_done, 2 * NC)
            pool.wait_ge(vg_ones, 1)

            def take_values(unit, par):
                if not isinstance(unit, int) or unit >= 1:
                    loop_wait(pool, pv_done, (unit - 1) * NSTEP + 1)
                nc.gpsimd.tensor_copy(vg[:, par, :, :, 0:HD],
                                      v_all[:, :, bass.ds(unit, 1)].rearrange("p j o (h n) -> p (j o) h n", h=GH)
                                      ).then_inc(vg_done, 1)

            pool.wait_ge(xt_ps, 2 * NC)
            for n in range(1, KT - 1):
                i = KT - 2 - n
                first = v_all[:, KT - 1] if n == 1 else w_sum(i + 1)
                if n > 1:
                    pool.wait_ge(wsum_done, n - 1)
                if n > 2:
                    pool.wait_ge(suf_ps, n)
                nc.gpsimd.tensor_tensor(w_sum(i), first, v_all[:, i + 1], ALU.add).then_inc(wsum_done, 1)
            take_values(0, 0)

            def cut_maxima(unit, par, half):
                m = mneg[:, par, :, half * TPC:(half + 1) * TPC]
                base = unit * sum(CUTS) + half * CUTS[0]
                if half == 0:
                    if isinstance(unit, int) and unit == 0:
                        pool.wait_ge(ring_free, NA)
                    else:
                        loop_wait(pool, ring_free, ring_count(unit - 1, RED_A[-1]))
                    nc.gpsimd.tensor_scalar(m, mp[:, 0:NA].rearrange("p (i h) -> p h i", h=GH), MASKED / SCALE, -1.0,
                                            ALU.max, ALU.mult).then_inc(cut_step, 1)
                    base = base + 1
                    loop_wait(pool, cut_step, base)
                else:
                    loop_wait(pool, mneg_done, unit + 1)
                nc.gpsimd.tensor_copy(mpart[:, half, 0], m).then_inc(cut_step, 1)
                loop_wait(pool, cut_step, base + 1)
                nc.gpsimd.tensor_tensor(mres[:, half], m, mpart[:, half, 0], ALU.subtract).then_inc(cut_step, 1)
                loop_wait(pool, cut_step, base + 2)
                nc.gpsimd.tensor_copy(mpart[:, half, 1], mres[:, half]).then_inc(cut_step, 1)
                loop_wait(pool, cut_step, base + 3)
                nc.gpsimd.tensor_tensor(mpart[:, half, 2], mres[:, half], mpart[:, half, 1], ALU.subtract
                                        ).then_inc(mp_cut, 1)
                loop_wait(pool, mp_cut, unit * 2 + half + 1)

            def mask(step, s):
                loop_wait(pool, p_done, step * 2 + 2)
                tile = probs[:, s % RING, :, 0:P]
                nc.gpsimd.affine_select(out=tile, in_=tile, compare_op=ALU.is_ge, fill=0.0, base=0,
                                        pattern=[[0, GH], [1, P]], channel_multiplier=-1).then_inc(p_masked, 1)

            def masked_share(unit, par):
                nc.gpsimd.tensor_scalar(ea[:], mneg[:, par], SCALE, -MASKED, ALU.mult, ALU.min).then_inc(ea_step, 1)
                loop_wait(pool, ea_step, unit * 2 + 1)
                nc.gpsimd.tensor_scalar_add(ea[:], ea[:], MASKED).then_inc(ea_done, 1)
                loop_wait(pool, et_done, unit + 1)
                nc.gpsimd.tensor_tensor(ecnt[:, par], et[:, par], count[:].unsqueeze(1).broadcast_to([P, GH, KT]),
                                        ALU.mult).then_inc(ea_step, 1)
                loop_wait(pool, ea_step, unit * 2 + 2)
                nc.gpsimd.tensor_tensor(
                    em[:, par], suffix[:, :, bass.ds(unit, 1)].rearrange("p j o (h n) -> p (j o) h n", h=GH),
                    et[:, par].rearrange("p h t -> p t h").unsqueeze(3).broadcast_to([P, KT, GH, HD]),
                    ALU.mult).then_inc(em_done, 1)

            def scale_o(unit, c):
                oc = unit * 2 + c
                loop_wait(pool, rcp_done, oc + 1)
                nc.gpsimd.tensor_tensor(
                    o_tok[:, c * TPC:(c + 1) * TPC, bass.ds(unit, 1)].rearrange("p j o (h n) -> p (j o) h n", h=GH),
                    num[:], rcp[:].unsqueeze(3).broadcast_to([P, TPC, GH, HD]), ALU.mult).then_inc(o_done, 1)

            cut_maxima(0, 0, 0)
            for s in range(AHEAD):
                if s == AHEAD - 1:
                    cut_maxima(0, 0, 1)
                if s in DIAG:
                    mask(s, s)
            pool.wait_ge(suf_done, KT)

            def body(unit, par, last):
                for t in range(NSTEP if not last else NSTEP - AHEAD):
                    s = (AHEAD + t) % NSTEP
                    if t == NSTEP - 1:
                        cut_maxima(unit + 1, 1 - par, 1)
                    if s in DIAG:
                        mask(unit * NSTEP + (AHEAD + t), s)
                    if t == 0:
                        masked_share(unit, par)
                        if not last:
                            take_values(unit + 1, 1 - par)
                    if last and t == WO_SLOT + 1:
                        inverse_deviation("OUT", 0)
                    if t == 4:
                        if not last:
                            cut_maxima(unit + 1, 1 - par, 0)
                        scale_o(unit, 0)
                scale_o(unit, 1)

            with pool.Fori(0, UNITS // 2 - 1) as it:
                body(it * 2, 0, False)
                body(it * 2 + 1, 1, False)
            body(UNITS - 2, 0, False)
            body(UNITS - 1, 1, True)

            pool.wait_ge(o_done, UNITS * 2 + 1)
            for c in range(1, NC):
                pool.wait_ge(at_ps, c)
                b, j0 = c // 2, c % 2 * TPC
                nc.gpsimd.tensor_copy(o_now[:].rearrange("p j (g n) -> p j g n", g=GROUPS),
                                      o_tok[:, j0:j0 + TPC, b * GROUPS:(b + 1) * GROUPS, :]).then_inc(o_taken, 1)
                inverse_deviation("OUT", c)


def constants():
    p = np.arange(P)
    bits = p[:, None] & p[None, :]
    odd = np.zeros((P, P), np.int64)
    for b in range(P.bit_length()):
        odd ^= (bits >> b) & 1
    floor = np.full((P, GH, KT // 2), -MASKED / SCALE, np.float32)
    floor[P - 1, :, KT // 2 - 1] = 3e38
    return {
        "had": (1.0 - 2.0 * odd).astype(np.float32),
        "ident": np.eye(P, dtype=np.float32),
        "tri": np.where(p[None, :] > p[:, None], NEG_BIG, 0.0).astype(np.float32),
        "after": (p[:, None] > p[None, :]).astype(np.float32),
        "count": (SEQ - 1 - (p[:, None] + P * np.arange(KT)[None, :])).astype(np.float32),
        "floor": floor,
    }


def kernel(L0_attn_x, L0_attn_Wqkv, L0_attn_bqkv, L0_attn_Wo, L0_attn_bo, L0_ffn_W1, L0_ffn_W2, L0_ffn_W3):
    import concourse.bacc as bacc
    from concourse.bass_utils import run_bass_kernel_spmd

    bqkv = np.asarray(L0_attn_bqkv)
    arrays = {
        "x": np.ascontiguousarray(np.asarray(L0_attn_x).reshape(TOKENS, D)),
        "w1t": np.ascontiguousarray(np.asarray(L0_ffn_W1).T),
        "w3t": np.ascontiguousarray(np.asarray(L0_ffn_W3).T),
        "w2t": np.ascontiguousarray(np.asarray(L0_ffn_W2).T),
        "wqkv": np.ascontiguousarray(np.asarray(L0_attn_Wqkv)),
        "wo": np.ascontiguousarray(np.asarray(L0_attn_Wo)),
        "bqk": np.ascontiguousarray(bqkv[:2 * D].reshape(4, P).T),
        "bv": np.ascontiguousarray(bqkv[2 * D:].reshape(1, D)),
        "bo": np.ascontiguousarray(np.asarray(L0_attn_bo).reshape(1, D)),
        **constants(),
    }
    nc = bacc.Bacc("TRN2", target_bir_lowering=False, num_devices=1)
    args = [nc.dram_tensor("in_" + n, a.shape, mybir.dt.from_np(a.dtype), kind="ExternalInput").ap() for n, a in arrays.items()]
    out = nc.dram_tensor("out_tokens", (TOKENS, D), F32, kind="ExternalOutput").ap()
    macaron(nc, *args, out)
    r = run_bass_kernel_spmd(nc, [{"in_" + n: a for n, a in arrays.items()}], core_ids=[0])
    return r.results[0]["out_tokens"].reshape(BATCH, SEQ, D)
```

```python
from contextlib import ExitStack

import numpy as np

import concourse.bass as bass
from concourse import mybir

F32 = mybir.dt.float32
F32R = mybir.dt.float32r
BF16 = mybir.dt.bfloat16
ACT = mybir.ActivationFunctionType
ALU = mybir.AluOpType
AX = mybir.AxisListType

P = 128
BATCH, SEQ, D = 2, 1024, 256
HIDDEN = 1024
HEADS, HD = 16, 16
TOKENS = BATCH * SEQ
CH = 512
NC = TOKENS // CH
TPC = CH // P
ND = D // P
NH = HIDDEN // P
GH = 4
GROUPS = HEADS // GH
UNITS = BATCH * GROUPS
KT = SEQ // P
VW = 32
PARTS = 3
SINGLES = ((0, 1), (1, 0), (0, 0))
STAGED = (lambda part: part, lambda part: PARTS - 1 - part)
STACK_LOADS = 2 * (1 + len(SINGLES))
QBUF = 4
SROWS = (PARTS + len(SINGLES)) * HD
MROWS = SROWS + PARTS
EPS = 1e-5
SCALE = 1.0 / float(np.sqrt(HD))
MASKED = -10000.0
NEG_BIG = -1e30

STEPS = [(c, j, max(0, j * P - c * CH)) for c in range(2) for j in range(KT) if j * P < (c + 1) * CH]
NSTEP = len(STEPS)
STEPS_C0 = sum(1 for s in STEPS if s[0] == 0)
SLOT_BASE = 2000
AHEAD = 3
DIAG = [s for s, (c, j, q0) in enumerate(STEPS) if j * P >= c * CH]

def red_width(i, piece):
    return min(CH, (i + 1) * P - piece * CH)


def red_heads(i, piece):
    return {P: 4, 2 * P: 2}.get(red_width(i, piece), 1)


RED_A, RED_B = [[("red", i, h, piece) for i in tiles for piece in range(1 + i // TPC) for h in range(0, GH, red_heads(i, piece))]
                for tiles in (range(KT // 2), range(KT // 2, KT))]
MA = KT // 2 * GH
NA = len(RED_A)
RING = 3

W2_SCALE = 0.5 / float(np.sqrt(HIDDEN))


def loop_wait(eng, sem, value):
    eng.wait_ge(sem, value)
    if not isinstance(value, int):
        eng.nop(nofuse=True)


def body_plan():
    reds = [(it, red_heads(it[1], it[3]) * red_width(it[1], it[3]) + 120) for it in RED_A + RED_B]
    room = [CH - STEPS[(AHEAD + t) % NSTEP][2] + SLOT_BASE for t in range(NSTEP - 1)]
    total = 1.05 * sum(w for _, w in reds)
    slots = [[] for _ in range(NSTEP)]
    done = 0
    for n, (it, w) in enumerate(reds):
        at = next(t for t in range(NSTEP - 1) if done * sum(room) < sum(room[:t + 1]) * total)
        slots[at].append(it)
        if n == NA + 4:
            slots[at].append(("mt", 0, 0, 0))
        done += w
    slots[STEPS_C0 - AHEAD + 2].append(("ot", 0, 0, 0))
    slots[NSTEP - AHEAD + 2] += [("ot", 1, 0, 0), ("mt", 1, 0, 0)]
    return slots


BODY = body_plan()
BODY_ITEMS = [it for s in BODY for it in s]
FIRST_ITEMS = RED_A + RED_B[:8] + [("mt", 0, 0, 0)] + RED_B[8:] + [("mt", 1, 0, 0)]
SUFFIX_FROM, SUFFIX_GAP = 6, 3
FIRST_GAP = 3
FIRST_SCORES = len(FIRST_ITEMS) - 1 - 2 * FIRST_GAP
LO_FIRST = 4
LAST_ITEMS = [("ot", 0, 0, 0), ("ot", 1, 0, 0)]
NBODY, NFIRST = len(BODY_ITEMS), len(FIRST_ITEMS)
RING_TOTAL = NFIRST + (UNITS - 1) * NBODY + len(LAST_ITEMS)


def ring_count(unit, item):
    items = LAST_ITEMS if isinstance(unit, int) and unit == UNITS - 1 else BODY_ITEMS
    return unit * NBODY + (NFIRST + items.index(item) + 1)


def macaron(nc, x_d, w1t_d, w3t_d, w2t_d, wqkv_d, wo_d, bqk_d, bv_d, bo_d, had_d, ident_d, tri_d,
            after_d, count_d, floor_d, out_d):
    ctx = ExitStack()
    with ctx:
        def sb(name, shape, dt):
            return ctx.enter_context(nc.sbuf_tensor(name, shape, dt))

        def sem(name):
            return ctx.enter_context(nc.semaphore(name))

        x = sb("x", [P, NC * TPC, D], F32)
        w1 = sb("w1", [P, 2, ND, HIDDEN], F32R)
        w3 = sb("w3", [P, 2, ND, HIDDEN], F32R)
        w2 = sb("w2", [P, 2, NH, D], F32R)
        wo = sb("wo", [P, 2, ND, D], F32R)
        v_all = sb("v_all", [P, KT, UNITS, GH * HD], F32)

        def take_turns(*groups):
            made = []
            for g in groups[1:]:
                with ExitStack() as s:
                    made.append([s.enter_context(nc.sbuf_tensor(n, sh, t)) for n, sh, t in g])
            return [[sb(n, sh, t) for n, sh, t in groups[0]]] + made

        (xt,), (v_split, probs) = take_turns([("xt", [P, NC, 2, ND, CH], F32R)],
                                       [("v_split", [P, 2, 2, UNITS * GH * HD], F32R), ("probs", [P, RING, GH, CH], F32)])
        (qs, ks), (w1_raw, w3_raw, w2_raw, wqkv_raw, wo_raw), (xa,) = take_turns(
            [("qs", [MROWS, 2, 2, GH, CH], BF16), ("ks", [MROWS, 2, 2, GH, CH], BF16)],
            [("w1_raw", [P, ND, HIDDEN], F32), ("w3_raw", [P, ND, HIDDEN], F32), ("w2_raw", [P, NH, D], F32),
             ("wqkv_raw", [P, ND, 3 * D], F32), ("wo_raw", [P, ND, D], F32)],
            [("xa", [P, 2, ND, CH], F32R)])
        (o_tok,), (wqkv, qf) = take_turns([("o_tok", [P, KT, UNITS, GH * HD], F32)],
                                          [("wqkv", [P, 2, ND, 3 * D], F32R), ("qf", [P, 2, CH], F32)])
        (u, uh, ul), (vg, o_raw, num) = take_turns(
            [("u", [P, 2, CH], F32), ("uh", [P, 2, CH], F32R), ("ul", [P, 2, CH], F32R)],
            [("vg", [P, 2, KT, GH, VW], F32), ("o_raw", [P, CH], F32), ("num", [P, TPC, GH, HD], F32)])
        (suffix,), (o_now,), (r1, stage) = take_turns(
            [("suffix", [P, KT, UNITS, GH * HD], F32)],
            [("o_now", [P, TPC, D], F32)],
            [("r1", [P, 2, CH], F32), ("stage", [P, QBUF, PARTS, CH], BF16)])
        (xn,), (v_third,) = take_turns([("xn", [P, TPC, D], F32)], [("v_third", [P, 2, UNITS * GH * HD], F32R)])
        had = sb("had", [P, P], F32)
        ident = sb("ident", [P, P], F32)
        sides_f = sb("sides_f", [P, 2, P], F32)
        sides = sb("sides", [P, 2, P], F32R)
        ident_b = sb("ident_b", [P, P], BF16)
        tri_f = sb("tri_f", [P, P], F32)
        tri_b = sb("tri_b", [P, P], BF16)
        bqk = sb("bqk", [P, 4], F32)
        bv = sb("bv", [P, D], F32)
        bo = sb("bo", [P, D], F32)
        count = sb("count", [P, KT], F32)
        neg_floor = sb("neg_floor", [P, GH, KT // 2], F32)
        bn = sb("bn", [P, TPC, 6], F32)
        mv = sb("mv", [P, TPC, 2], F32)
        ve = sb("ve", [P, TPC], F32)
        rstd = sb("rstd", [P, TPC], F32)
        neg_half = sb("neg_half", [P, TPC], F32)
        mp = sb("mp", [P, 3 * MA], F32)
        mb = sb("mb", [P, GH, KT // 2], F32)
        mneg = sb("mneg", [P, 2, GH, KT], F32)
        mres = sb("mres", [P, 2, GH, KT // 2], F32)
        mpart = sb("mpart", [P, 2, PARTS, GH, KT // 2], BF16)
        MT = GH * KT // 2
        mt = sb("mt", [PARTS * MT, 2, P], BF16)
        ea = sb("ea", [P, GH, KT], F32)
        et = sb("et", [P, 2, GH, KT], F32)
        ecnt = sb("ecnt", [P, GH, KT], F32)
        em = sb("em", [P, KT, GH, HD], F32)
        dsum = sb("dsum", [P, TPC, GH], F32)
        rcp = sb("rcp", [P, TPC, GH], F32)

        banks = [ctx.enter_context(nc.psum_tensor(f"bank{i}", [P, CH], F32)) for i in range(4)]
        pair = [ctx.enter_context(nc.psum_tensor(f"pair{i}", [P, 2, CH], F32)) for i in range(2)]
        ps_gate, ps_lin = banks[0:2], banks[2:4]
        ps_down, ps_t = pair
        ps_ring, ps_o, ps_s = banks[0:3], banks[3], pair
        T_BANKS = [ps_t[:, d, :] for d in range(2)]
        FREE_BANKS = [t[:] for t in banks[1:3]]

        parts_d = nc.dram_tensor("parts", (2, UNITS, 2, GH * HD, PARTS, CH), BF16, kind="Internal").ap()

        ld_x = [sem(f"ld_x{c}") for c in range(NC)]
        ld_w1, ld_w3 = [[sem(f"ld_{w}_{i}") for i in range(2)] for w in ("w1", "w3")]
        ld_w2, ld_ident, ld_had = sem("ld_w2"), sem("ld_ident"), sem("ld_had")
        ld_wqkv, ld_wo, ld_const = sem("ld_wqkv"), sem("ld_wo"), sem("ld_const")
        const_cut, pool_const, stack_ones, vg_ones = sem("const_cut"), sem("pool_const"), sem("stack_ones"), sem("vg_ones")
        bn_done, mv_done, ve_done = sem("bn_done"), sem("mv_done"), sem("ve_done")
        rstd_done, xn_done = sem("rstd_done"), sem("xn_done")
        xt_ps, xt_hi, xt_lo = sem("xt_ps"), sem("xt_hi"), sem("xt_lo")
        w13_hi, w13_lo, fly_sum, fly_diff = sem("w13_hi"), sem("w13_lo"), sem("fly_sum"), sem("fly_diff")
        had_ps, w2_hi, w2_lo = sem("had_ps"), sem("w2_hi"), sem("w2_lo")
        wsplit_hi, wsplit_lo = sem("wsplit_hi"), sem("wsplit_lo")
        gate_done, lin_done, silu_done = sem("gate_done"), sem("lin_done"), sem("silu_done")
        u_done, uh_done, ul_done = sem("u_done"), sem("uh_done"), sem("ul_done")
        down_used, down_done, res_added = sem("down_used"), sem("down_done"), sem("res_added")
        qk_ps, qf_done, qh_done, r1_done = sem("qk_ps"), sem("qf_done"), sem("qh_done"), sem("r1_done")
        qm_done, ql_done, v_ps, v_done = sem("qm_done"), sem("ql_done"), sem("v_ps"), sem("v_done")
        part_out = [sem(f"part_out{i}") for i in range(QBUF)]
        stack_in = [sem(f"stack_in{i}") for i in range(2)]
        mrow_in = [sem(f"mrow_in{i}") for i in range(2)]
        vs_hi, vs_lo, suf_ps, suf_done = sem("vs_hi"), sem("vs_lo"), sem("suf_ps"), sem("suf_done")
        vg_done, bo_added, o_taken = sem("vg_done"), sem("bo_added"), sem("o_taken")
        at_ps, at_hi, at_lo, wo_done, att_added = (sem("at_ps"), sem("at_hi"), sem("at_lo"), sem("wo_done"),
                                                   sem("att_added"))
        ring_full, ring_free = sem("ring_full"), sem("ring_free")
        mb_done, mneg_done, front_done = sem("mb_done"), sem("mneg_done"), sem("front_done")
        cut_step, mp_cut = [[sem(f"{n}{half}") for half in range(2)] for n in ("cut_step", "mp_cut")]
        ea_step, ea_done, et_done, em_done = sem("ea_step"), sem("ea_done"), sem("et_done"), sem("em_done")
        s_ps, p_done, p_masked, pv_done = sem("s_ps"), sem("p_done"), sem("p_masked"), sem("pv_done")
        o_copied, dsum_done, rcp_done, o_done = sem("o_copied"), sem("dsum_done"), sem("rcp_done"), sem("o_done")
        out_sent = sem("out_sent")

        ORDER = {"IN": 0, "FF": NC, "OUT": 2 * NC}

        def fill_no(kind, c):
            return ORDER[kind] + c

        RES = {"FF": 0, "FF2": NC}
        WSPLIT = 4
        WP = HIDDEN // WSPLIT

        def chunk_of(t, c):
            return t[:, bass.ds(c * TPC, TPC), :]

        AT_SLOT, WO_SLOT, OUT_SLOT = 0, 2, 6
        LOADS_EACH = 3
        LAST_FILL = 4
        def split_values(n, part):
            return v_third[:, part] if n % 3 == 2 else v_split[:, part, n % 3]

        CUTS = 3

        def fly_views(stage_no):
            fly = v_all[:, 0:NH // 2].rearrange("p j u n -> p (j u n)").rearrange("p (k n) -> p k n", n=D)
            places = (w2_raw[:], fly) if stage_no % 2 == 0 else (fly, w2_raw[:])
            src, dst = [t.rearrange("p (a two b) n -> p two a (b n)", two=2, b=1 << stage_no) for t in places]
            return src[:, 0], src[:, 1], dst[:, 0], dst[:, 1]

        def cut_maxima(ops, wait, unit, par, half):
            m = mneg[:, par, :, half * TPC:(half + 1) * TPC]
            base = unit * CUTS
            ops.tensor_copy(mpart[:, half, 0], m).then_inc(cut_step[half], 1)
            wait(cut_step[half], base + 1)
            ops.tensor_tensor(mres[:, half], m, mpart[:, half, 0], ALU.subtract).then_inc(cut_step[half], 1)
            wait(cut_step[half], base + 2)
            ops.tensor_copy(mpart[:, half, 1], mres[:, half]).then_inc(cut_step[half], 1)
            wait(cut_step[half], base + 3)
            ops.tensor_tensor(mpart[:, half, 2], mres[:, half], mpart[:, half, 1], ALU.subtract).then_inc(mp_cut[half], 1)

        def staged(k, part):
            return STAGED[k % 4 // 2](part)

        def sent(projections, buf):
            return 16 * len(range(buf, projections, QBUF))

        def fly_out(i):
            return v_all[:, i].rearrange("p u n -> p (u n)")

        block = ctx.enter_context(nc.Block())

        @block.sync
        def _(sp):
            x_t = x_d.rearrange("(t p) n -> p t n", p=P)
            sp.dma_start(x[:, 0:TPC, :], x_t[:, 0:TPC, :]).then_inc(ld_x[0], 16)
            sp.dma_start(w2_raw[:], w2t_d.rearrange("(c p) n -> p c n", p=P)).then_inc(ld_w2, 16)
            sp.dma_start(ident[:], ident_d).then_inc(ld_ident, 16)
            for i in range(2):
                cols = slice(i * HIDDEN // 2, (i + 1) * HIDDEN // 2)
                for raw, w_d, loaded in ((w1_raw, w1t_d, ld_w1), (w3_raw, w3t_d, ld_w3)):
                    sp.dma_start(raw[:, :, cols], w_d.rearrange("(c p) n -> p c n", p=P)[:, :, cols]).then_inc(loaded[i], 16)
                if i == 0:
                    sp.dma_start(had[:], had_d).then_inc(ld_had, 16)
                    sp.dma_start(chunk_of(x, 1), chunk_of(x_t, 1)).then_inc(ld_x[1], 16)
            for c in range(2, NC):
                sp.dma_start(chunk_of(x, c), chunk_of(x_t, c)).then_inc(ld_x[c], 16)
            sp.dma_start(wqkv_raw[:], wqkv_d.rearrange("(c p) n -> p c n", p=P)).then_inc(ld_wqkv, 16)
            sp.dma_start(wo_raw[:], wo_d.rearrange("(c p) n -> p c n", p=P)).then_inc(ld_wo, 16)
            for t, d_ in ((bqk, bqk_d), (neg_floor, floor_d), (tri_f, tri_d), (sides_f, after_d), (count, count_d),
                          (bv, bv_d.broadcast_to([P, D])), (bo, bo_d.broadcast_to([P, D]))):
                sp.dma_start(t[:], d_).then_inc(ld_const, 16)

            def send_parts(k):
                c, ct = k // 4, k % 4
                sp.wait_ge(ql_done, k + 1)
                unit = (c // 2) * GROUPS + (ct % 2) * 2
                sp.dma_start(parts_d[ct // 2, unit:unit + 2, c % 2].rearrange("u r a t -> u r (a t)"),
                             stage[:, k % QBUF].rearrange("p a t -> p (a t)")).then_inc(part_out[k % QBUF], 16)

            def load_stack(unit, slot, loads=range(STACK_LOADS)):
                for load in loads:
                    which, n = load % 2, load // 2
                    src, stack = parts_d[which, bass.ds(unit, 1)], (qs, ks)[which]
                    if n == 0:
                        rows = slice(0, PARTS * HD)
                        src = src.rearrange("u s (h r) a t -> (r a) (u s h) t", r=HD)
                    else:
                        rows = slice((PARTS + n - 1) * HD, (PARTS + n) * HD)
                        place = STAGED[which](SINGLES[n - 1][which])
                        src = src[:, :, :, place, :].rearrange("u s (h r) t -> r (u s h) t", r=HD)
                    sp.dma_start(stack[rows, slot].rearrange("r s h t -> r (s h) t"), src).then_inc(stack_in[slot], 16)

            def load_max_rows(items, slot, half):
                sp.wait_ge(ring_free, items)
                sp.dma_start(qs[SROWS:MROWS, slot, half].rearrange("p h (t q) -> p (h t) q", q=P), mt[:, half, :]
                             ).then_inc(mrow_in[half], 16)

            for k in range(2 * NC + 2):
                send_parts(k)
            for n in range(QBUF):
                sp.wait_ge(part_out[n], sent(2 * NC, n))
            sp.wait_ge(wsplit_lo, 2)
            sp.wait_ge(w2_lo, NH // 2)
            sp.wait_ge(w13_lo, 2 * WSPLIT)
            for k in range(2 * NC + 2, 4 * NC):
                n = k - (2 * NC + 2)
                load_stack(0, 0, range(STACK_LOADS)[LOADS_EACH * n:LOADS_EACH * n + LOADS_EACH])
                send_parts(k)
            load_stack(1, 1)
            for n in range(QBUF):
                sp.wait_ge(part_out[n], sent(4 * NC, n))
            for half in range(2):
                load_max_rows(FIRST_ITEMS.index(("mt", half, 0, 0)) + 1, 0, half)

            def body(unit, par, more):
                load_max_rows(ring_count(unit, ("mt", 0, 0, 0)), 1 - par, 0)
                if more:
                    sp.wait_ge(s_ps, (unit + 1) * (2 * NSTEP))
                    load_stack(unit + 2, par)
                load_max_rows(ring_count(unit, ("mt", 1, 0, 0)), 1 - par, 1)

            with sp.Fori(0, UNITS // 2 - 1) as it:
                body(it * 2, 0, True)
                body(it * 2 + 1, 1, True)
            body(UNITS - 2, 0, False)

            for c in range(NC):
                sp.wait_ge(res_added, RES["FF2"] + c + 1)
                sp.dma_start(chunk_of(out_d.rearrange("(t p) n -> p t n", p=P), c), chunk_of(x, c)
                             ).then_inc(out_sent, 16)
            sp.wait_ge(out_sent, 16 * NC)

        @block.tensor
        def _(pe):
            PASSES = ((0, 0), (0, 1), (1, 0))

            def transposes(place, src, done):
                for d in range(ND):
                    for t in range(TPC):
                        last = nc.tensor.transpose(place[d][:, t * P:(t + 1) * P], src(t, d), ident[:])
                last.then_inc(done, 1)

            def norm_transposes(kind, c, place=T_BANKS):
                n = fill_no(kind, c)
                pe.wait_ge(xn_done, n + 1)
                if place is T_BANKS and (not isinstance(n, int) or n > 0):
                    pe.wait_ge(xt_hi, n)
                    pe.wait_ge(xt_lo, n)
                transposes(place, lambda t, d: xn[:, t, d * P:(d + 1) * P], xt_ps)

            def att_transposes(c):
                if isinstance(c, int) and c == 0:
                    pe.wait_ge(o_done, GROUPS * 2)
                    transposes(FREE_BANKS, lambda t, d: o_tok[:, t, 2 * d:2 * d + 2, :].rearrange("p g n -> p (g n)"), at_ps)
                else:
                    pe.wait_ge(o_taken, c)
                    pe.wait_ge(xt_hi, fill_no("OUT", c))
                    pe.wait_ge(xt_lo, fill_no("OUT", c))
                    transposes(T_BANKS, lambda t, d: o_now[:, t, d * P:(d + 1) * P], at_ps)

            def output_projection(c, place=T_BANKS):
                pe.wait_ge(at_lo, c + 1)
                pe.wait_ge(at_hi, c + 1)
                for t in range(TPC):
                    for n, (d, (wp, xp)) in enumerate([(d, p) for d in range(ND) for p in PASSES]):
                        last = nc.tensor.matmul(place[t // 2][:, (t % 2) * D:(t % 2 + 1) * D],
                                                xa[:, xp, d, t * P:(t + 1) * P], wo[:, wp, d, :],
                                                start=n == 0 and t % 2 == 0, stop=n == 5, skip_group_check=True)
                last.then_inc(wo_done, 1)

            def up(k, c, hc):
                for ps, w, freed, done in ((ps_gate, w1, silu_done, gate_done), (ps_lin, w3, u_done, lin_done)):
                    if not isinstance(k, int) or k >= 2:
                        pe.wait_ge(freed, k - 1)
                    n = 0
                    for d in range(ND):
                        for wp, xp in PASSES:
                            last = nc.tensor.matmul(ps[hc % 2][:], w[:, wp, d, hc * P:(hc + 1) * P],
                                                    xt[:, bass.ds(c, 1), xp, d, :].rearrange("p o t -> p (o t)"),
                                                    start=n == 0, stop=n == 5)
                            n += 1
                    last.then_inc(done, 1)

            def down(k, hc, chunks_before):
                pe.wait_ge(ul_done, k + 1)
                if hc == 0 and (not isinstance(chunks_before, int) or chunks_before > 0):
                    pe.wait_ge(res_added, chunks_before)
                for t in range(TPC):
                    for n, (wp, up_) in enumerate(PASSES):
                        lhs = (uh, ul)[up_]
                        last = nc.tensor.matmul(ps_down[:, t // 2, (t % 2) * D:(t % 2 + 1) * D],
                                                lhs[:, hc % 2, t * P:(t + 1) * P], w2[:, wp, hc, :],
                                                start=hc == 0 and n == 0 and t % 2 == 0,
                                                stop=hc == NH - 1 and n == 2, skip_group_check=True)
                last.then_inc(down_done if hc == NH - 1 else down_used, 1)

            def feed_forward(layer, fills, c, before, extra):
                k0 = (layer * NC + c) * NH
                res = (RES["FF"], RES["FF2"])[layer] + c
                pe.wait_ge(xt_lo, fills)
                pe.wait_ge(xt_hi, fills)
                for hc in range(NH):
                    if hc > 0 or not (isinstance(c, int) and (layer, c) == (1, 0)):
                        up(k0 + hc, c, hc)
                    if hc == 0:
                        before()
                    else:
                        down(k0 + hc - 1, hc - 1, res)
                    extra(hc)

            def last_down(layer, c):
                down((layer * NC + c) * NH + NH - 1, NH - 1, 0)

            pe.wait_ge(ld_ident, 16)
            norm_transposes("IN", 0)

            def hadamard(i):
                if i == 0:
                    pe.wait_ge(ld_had, 16)
                    pe.wait_ge(fly_sum, 3)
                    pe.wait_ge(fly_diff, 3)
                if i >= 2:
                    pe.wait_ge(w2_lo, i - 1)
                nc.tensor.matmul(ps_down[:, i % 2, :], had[:], fly_out(i),
                                 start=True, stop=True).then_inc(had_ps, 1)

            def first_extra(hc):
                if hc < 2:
                    hadamard(2 * hc)
                    hadamard(2 * hc + 1)
                if hc == 1:
                    pe.wait_ge(w2_lo, NH // 2)
                    pe.wait_ge(w2_hi, NH // 2)
                if hc in (2, 4, 6):
                    norm_transposes("IN", hc // 2)

            pe.wait_ge(xt_lo, 1)
            pe.wait_ge(xt_hi, 1)
            for hc in range(NH):
                if hc % 2 == 0:
                    pe.wait_ge(w13_lo, hc + 2)
                    pe.wait_ge(w13_hi, hc + 2)
                up(hc, 0, hc)
                first_extra(hc)
                if hc >= 1:
                    down(hc - 1, hc - 1, 0)

            with pe.Fori(1, NC) as c:
                feed_forward(0, fill_no("IN", c) + 1, c, lambda: last_down(0, c - 1),
                             lambda hc: norm_transposes("FF", c - 1) if hc == 3 else None)
            last_down(0, NC - 1)

            pe.wait_ge(silu_done, NC * NH)
            pe.wait_ge(u_done, NC * NH)
            pe.wait_ge(wsplit_lo, 2)
            for c in range(NC):
                pe.wait_ge(xt_lo, fill_no("FF", c) + 1)
                pe.wait_ge(xt_hi, fill_no("FF", c) + 1)
                for ct in range(4):
                    k = 4 * c + ct
                    if k >= 2:
                        pe.wait_ge(qf_done, k - 1)
                    for n, (d, (wp, xp)) in enumerate([(d, p) for d in range(ND) for p in PASSES]):
                        last = nc.tensor.matmul(banks[k % 2][:], wqkv[:, wp, d, ct * P:(ct + 1) * P],
                                                xt[:, c, xp, d, :], start=n == 0, stop=n == 5)
                    last.then_inc(qk_ps, 1)
                for vv in range(2):
                    i = 2 * c + vv
                    if i >= 2:
                        pe.wait_ge(v_done, i - 1)
                    for tt in range(2):
                        t = 2 * vv + tt
                        for n, (d, (wp, xp)) in enumerate([(d, p) for d in range(ND) for p in PASSES]):
                            last = nc.tensor.matmul(banks[2 + i % 2][:, tt * D:(tt + 1) * D],
                                                    xt[:, c, xp, d, t * P:(t + 1) * P], wqkv[:, wp, d, 2 * D:3 * D],
                                                    start=tt == 0 and n == 0, stop=n == 5, skip_group_check=True)
                    last.then_inc(v_ps, 1)
                if c == 0:
                    norm_transposes("FF", NC - 1)

            def suffix_sums(n):
                pe.wait_ge(vs_hi, n + 1)
                pe.wait_ge(vs_lo, n + 1)
                if n > 0:
                    pe.wait_ge(suf_done, n)
                    for part in range(2):
                        nc.tensor.matmul(ps_down[:, 0, :], sides[:, 1], split_values(n - 1, part), start=False,
                                         stop=False, skip_group_check=True)
                for part in range(2):
                    last = nc.tensor.matmul(ps_down[:, 0, :], sides[:, 0], split_values(n, part),
                                            start=n == 0 and part == 0, stop=part == 1, skip_group_check=True)
                last.then_inc(suf_ps, 1)

            def ring_item(item, bank, free_at, unit, par, prev_unit):
                kind, a, h, piece = item
                out = ps_ring[bank]
                if free_at is not None:
                    pe.wait_ge(ring_free, free_at)
                if kind == "red":
                    n = red_width(a, piece)
                    diagonal = piece == a // TPC
                    for k in range(red_heads(a, piece)):
                        last = nc.tensor.matmul(out[:, k * n:(k + 1) * n],
                                                qs[0:SROWS, par, a // TPC, h + k, (a % TPC) * P:(a % TPC + 1) * P],
                                                ks[0:SROWS, par, piece, h + k, 0:n], start=k == 0, stop=not diagonal,
                                                skip_group_check=True)
                    if diagonal:
                        for k in range(red_heads(a, piece)):
                            last = nc.tensor.matmul(out[:, (k + 1) * n - P:(k + 1) * n], ident_b[:], tri_b[:], start=False,
                                                    stop=True, skip_group_check=True)
                elif kind == "mt":
                    loop_wait(pe, mp_cut[a], unit + 1)
                    last = nc.tensor.transpose(out[0:PARTS * MT, 0:P // 2].bitcast(BF16),
                                               mpart[:, a].rearrange("p c h t -> p (c h t)"), ident_b[:])
                else:
                    pe.wait_ge(o_copied, prev_unit * 2 + a + 1)
                    for t in range(TPC):
                        last = nc.tensor.transpose(out[:, t * P:(t + 1) * P], o_raw[:, t * P:(t + 1) * P], ident[:])
                last.then_inc(ring_full, 1)

            def scores(step, s, p, par, unit):
                c, j, q0 = STEPS[s]
                if p == 0 and s in (0, STEPS_C0):
                    pe.wait_ge(mrow_in[c], (unit + 1) * 16)
                if not isinstance(step, int) or step > 0:
                    pe.wait_ge(p_done, step * 2 - 1 + p)
                for hh in range(2):
                    h = 2 * p + hh
                    last = nc.tensor.matmul(ps_s[p][:, hh, 0:CH - q0], ks[:, par, j // TPC, h, (j % TPC) * P:(j % TPC + 1) * P],
                                            qs[:, par, c, h, q0:CH], start=True, stop=True)
                last.then_inc(s_ps, 1)

            def values(step, s, par, unit):
                c, j, q0 = STEPS[s]
                pe.wait_ge(p_done, step * 2 + 2)
                if s in DIAG:
                    pe.wait_ge(p_masked, unit * len(DIAG) + (DIAG.index(s) + 1))
                if s == 0:
                    pe.wait_ge(vg_done, unit + 1)
                if s in (0, STEPS_C0) and (not isinstance(unit, int) or unit * 2 + c > 0):
                    pe.wait_ge(o_copied, unit * 2 + c)
                for h in range(GH):
                    last = nc.tensor.matmul(ps_o[VW * h:VW * (h + 1), q0:CH], vg[:, par, j, h, :],
                                            probs[:, s % RING, h, 0:CH - q0], start=j == 0,
                                            stop=j * P == (c + 1) * CH - P, tile_position=(0, VW * h),
                                            skip_group_check=True)
                last.then_inc(pv_done, 1)

            def first_scores(s):
                for p in range(2):
                    scores(s, s, p, 0, 0)
                if s > 0:
                    values(s - 1, s - 1, 0, 0)

            pe.wait_ge(qf_done, 4 * NC)
            pe.wait_ge(v_done, 2 * NC)
            pe.wait_ge(stack_ones, 1)
            pe.wait_ge(const_cut, 3)
            pe.wait_ge(stack_in[0], 16 * STACK_LOADS)
            for n, item in enumerate(FIRST_ITEMS):
                if n == FIRST_SCORES:
                    pe.wait_ge(suf_done, KT)
                if n >= FIRST_SCORES and (n - FIRST_SCORES) % FIRST_GAP == 0 and (n - FIRST_SCORES) // FIRST_GAP < AHEAD:
                    first_scores((n - FIRST_SCORES) // FIRST_GAP)
                ring_item(item, (n + 2) % RING, n - 2 if n >= RING else None, 0, 0, None)
                if (n - SUFFIX_FROM) % SUFFIX_GAP == 0 and 0 <= (n - SUFFIX_FROM) // SUFFIX_GAP < KT:
                    suffix_sums((n - SUFFIX_FROM) // SUFFIX_GAP)

            def body(unit, par, visit, last):
                ring0 = NFIRST + unit * NBODY
                pos = 0
                if not last:
                    pe.wait_ge(stack_in[1 - par], visit * (16 * STACK_LOADS))
                for t in range(NSTEP if not last else NSTEP - AHEAD):
                    s = (AHEAD + t) % NSTEP
                    step = unit * NSTEP + (AHEAD + t)
                    here = t < NSTEP - AHEAD
                    items = BODY[t] if not last else [i for i in BODY[t] if i[0] == "ot"]
                    if last and t == AT_SLOT:
                        pe.wait_ge(ring_free, ring0)
                        att_transposes(0)
                    if last and t == WO_SLOT:
                        output_projection(0, FREE_BANKS)
                    if last and t == OUT_SLOT:
                        norm_transposes("OUT", 0, FREE_BANKS)
                    for p in range(2):
                        scores(step, s, p, par if here else 1 - par, unit if here else unit + 1)
                        for item in (items[:len(items) - len(items) // 2], items[len(items) - len(items) // 2:])[p]:
                            if last:
                                free_at = ring0 + pos
                            else:
                                free_at = ring0 + (pos - 2 if pos >= RING else (0, -2, -1)[pos])
                            ring_item(item, pos % RING if not last else 0, free_at, unit + 1, 1 - par, unit)
                            pos += 1
                    was_here = t - 1 < NSTEP - AHEAD
                    values(step - 1, (s - 1) % NSTEP, par if was_here else 1 - par, unit if was_here else unit + 1)
                if last:
                    pe.wait_ge(xt_lo, fill_no("OUT", 0) + 1)
                    pe.wait_ge(xt_hi, fill_no("OUT", 0) + 1)
                    pe.wait_ge(ring_free, ring0 + pos)
                    up(NC * NH, 0, 0)
                    values(UNITS * NSTEP - 1, NSTEP - 1, par, unit)
                    ring_item(("ot", 1, 0, 0), 1, ring0 + pos, unit, par, unit)

            with pe.Fori(0, UNITS // 2 - 1) as it:
                body(it * 2, 0, it + 1, False)
                body(it * 2 + 1, 1, it + 2, False)
            body(UNITS - 2, 0, UNITS // 2, False)
            body(UNITS - 1, 1, None, True)

            pe.wait_ge(ring_free, RING_TOTAL)
            pe.wait_ge(p_done, 2 * NSTEP * UNITS)
            pe.wait_ge(o_copied, 2 * UNITS)

            def following(c):
                def extra(hc):
                    if hc == 0:
                        att_transposes(c)
                    if hc == 2:
                        output_projection(c)
                    if hc == 5:
                        norm_transposes("OUT", c)
                return extra

            feed_forward(1, fill_no("OUT", 0) + 1, 0, lambda: None, following(1))
            with pe.Fori(1, NC - 1) as c:
                feed_forward(1, fill_no("OUT", c) + 1, c, lambda: last_down(1, c - 1), following(c + 1))
            feed_forward(1, fill_no("OUT", NC - 1) + 1, NC - 1, lambda: last_down(1, NC - 2), lambda hc: None)
            last_down(1, NC - 1)

        @block.scalar
        def _(act):
            def at_fill_hi(c):
                act.wait_ge(at_ps, c + 1)
                for d in range(ND):
                    last = nc.scalar.copy(xa[:, 0, d, :], ps_t[:, d, :])
                last.then_inc(at_hi, 1)

            def fill_hi(kind, c):
                act.wait_ge(xt_ps, fill_no(kind, c) + 1)
                for d in range(ND):
                    last = nc.scalar.copy(xt[:, bass.ds(c, 1), 0, d, :].rearrange("p o t -> p (o t)"), ps_t[:, d, :])
                last.then_inc(xt_hi, 1)

            def w13_part(n):
                w, raw, loaded = ((w1, w1_raw, ld_w1), (w3, w3_raw, ld_w3))[n % 2]
                act.wait_ge(loaded[n // WSPLIT], 16)
                cols = slice((n // 2) * WP, (n // 2 + 1) * WP)
                nc.scalar.copy(w[:, 0, :, cols], raw[:, :, cols]).then_inc(w13_hi, 1)

            def gate(k, hc):
                act.wait_ge(gate_done, k + 1)
                if not isinstance(k, int) or k >= 2:
                    act.wait_ge(ul_done, k - 1)
                nc.scalar.activation(u[:, hc % 2, :], ps_gate[hc % 2][:], ACT.Silu).then_inc(silu_done, 1)

            def hidden_hi(k, hc, downs):
                act.wait_ge(u_done, k + 1)
                if downs is not None:
                    downs()
                nc.scalar.copy(uh[:, hc % 2, :], u[:, hc % 2, :]).then_inc(uh_done, 1)

            def downs_before(eng, layer, c, hc):
                if hc >= 2:
                    eng.wait_ge(down_used, (layer * NC + c) * (NH - 1) + hc - 1)
                elif isinstance(c, int) and c == 0 and layer == 0:
                    return
                elif hc == 0:
                    eng.wait_ge(down_used, (layer * NC + c) * (NH - 1))
                else:
                    eng.wait_ge(down_done, c + (RES["FF"], RES["FF2"])[layer])

            def feed_forward(layer, c, extra):
                for hc in range(NH):
                    k = (layer * NC + c) * NH + hc
                    gate(k, hc)
                    hidden_hi(k, hc, lambda: downs_before(act, layer, c, hc))
                    extra(hc)

            def w2_part(i):
                act.wait_ge(had_ps, i + 1)
                nc.scalar.activation(w2[:, 0, 2 * i:2 * i + 2, :], ps_down[:, i % 2, :].rearrange("p (a n) -> p a n", a=2),
                                     ACT.Copy, scale=W2_SCALE).then_inc(w2_hi, 1)

            w13_part(0)
            w13_part(1)
            fill_hi("IN", 0)
            for hc in range(NH):
                gate(hc, hc)
                if hc < 2:
                    w2_part(2 * hc)
                    w2_part(2 * hc + 1)
                hidden_hi(hc, hc, lambda: downs_before(act, 0, 0, hc))
                if hc < 3:
                    w13_part(2 * hc + 2)
                    w13_part(2 * hc + 3)
                if hc in (2, 4, 6):
                    fill_hi("IN", hc // 2)

            with act.Fori(1, NC) as c:
                feed_forward(0, c, lambda hc: fill_hi("FF", c - 1) if hc == 3 else None)

            act.wait_ge(ld_const, 16 * 7)
            def middle_part(k):
                act.wait_ge(r1_done, k + 1)
                nc.scalar.copy(stage[:, k % QBUF, staged(k, 1), :], r1[:, k % 2, :]).then_inc(qm_done, 1)

            for k in range(4 * NC):
                if k == LAST_FILL:
                    fill_hi("FF", NC - 1)
                act.wait_ge(qk_ps, k + 1)
                if k >= 2:
                    act.wait_ge(r1_done, k - 1)
                nc.scalar.activation(qf[:, k % 2, :], banks[k % 2][:], ACT.Identity,
                                     bias=bqk[:, k % 4:k % 4 + 1]).then_inc(qf_done, 1)
                act.wait_ge(qf_done, k + 1)
                if k >= QBUF:
                    act.wait_ge(part_out[k % QBUF], sent(k - QBUF + 1, k % QBUF))
                nc.scalar.copy(stage[:, k % QBUF, staged(k, 0), :], qf[:, k % 2, :]).then_inc(qh_done, 1)
                if k >= 1:
                    middle_part(k - 1)
            middle_part(4 * NC - 1)

            def value_hi(n):
                if n >= 3:
                    act.wait_ge(suf_ps, n - 1)
                nc.scalar.copy(split_values(n, 0), v_all[:, KT - 1 - n].rearrange("p u n -> p (u n)")).then_inc(vs_hi, 1)

            act.wait_ge(v_done, 2 * NC)
            act.wait_ge(xt_ps, 2 * NC)
            for n in range(3):
                value_hi(n)
            act.wait_ge(ql_done, 4 * NC)
            for n in range(QBUF):
                act.wait_ge(part_out[n], sent(4 * NC, n))
            for n in range(KT):
                act.wait_ge(suf_ps, n + 1)
                nc.scalar.copy(suffix[:, KT - 1 - n], ps_down[:, 0, :].rearrange("p (u n) -> p u n", u=UNITS)
                               ).then_inc(suf_done, 1)
                if 1 <= n < KT - 2:
                    value_hi(n + 2)

            def exponentials(step, s, p):
                c, j, q0 = STEPS[s]
                act.wait_ge(s_ps, step * 2 + p + 1)
                if p == 0 and (not isinstance(step, int) or step >= RING):
                    act.wait_ge(pv_done, step - (RING - 1))
                nc.scalar.activation(probs[:, s % RING, 2 * p:2 * p + 2, 0:CH - q0], ps_s[p][:, :, 0:CH - q0],
                                     ACT.Exp, scale=SCALE).then_inc(p_done, 1)

            def copy_o(unit, c):
                act.wait_ge(pv_done, unit * NSTEP + (STEPS_C0, NSTEP)[c])
                if c == 1:
                    act.wait_ge(ring_full, ring_count(unit, ("ot", 0, 0, 0)))
                elif not isinstance(unit, int) or unit > 0:
                    act.wait_ge(ring_full, (unit - 1) * NBODY + (NFIRST + BODY_ITEMS.index(("ot", 1, 0, 0)) + 1))
                nc.scalar.copy(o_raw[:], ps_o[:]).then_inc(o_copied, 1)

            for s in range(AHEAD):
                for p in range(2):
                    exponentials(s, s, p)

            def body(unit, par, last):
                for t in range(NSTEP if not last else NSTEP - AHEAD):
                    if t == 1:
                        act.wait_ge(ea_done, unit + 1)
                        nc.scalar.activation(et[:, par], ea[:], ACT.Exp).then_inc(et_done, 1)
                    if t == STEPS_C0 - AHEAD + 1:
                        copy_o(unit, 0)
                    if t == NSTEP - AHEAD + 1:
                        copy_o(unit, 1)
                    for p in range(2):
                        exponentials(unit * NSTEP + (AHEAD + t), (AHEAD + t) % NSTEP, p)
                if last:
                    copy_o(unit, 1)

            with act.Fori(0, UNITS // 2 - 1) as it:
                body(it * 2, 0, False)
                body(it * 2 + 1, 1, False)
            body(UNITS - 2, 0, False)
            body(UNITS - 1, 1, True)

            def following(c):
                def extra(hc):
                    if hc == 0:
                        at_fill_hi(c)
                    if hc == 5:
                        fill_hi("OUT", c)
                return extra

            feed_forward(1, 0, following(1))
            with act.Fori(1, NC - 1) as c:
                feed_forward(1, c, following(c + 1))
            feed_forward(1, NC - 1, lambda hc: None)

        @block.vector
        def _(dve):
            def statistics(kind, c):
                n = fill_no(kind, c)
                if not isinstance(n, int) or n > 0:
                    loop_wait(dve, rstd_done, n)
                for t in range(TPC):
                    last = nc.vector.bn_stats(bn[:, t, :], x[:, bass.ds(c * TPC + t, 1), :].rearrange("p o n -> p (o n)"))
                last.then_inc(bn_done, 1)
                loop_wait(dve, bn_done, n + 1)
                for t in range(TPC):
                    last = nc.vector.bn_aggr(mv[:, t, :], bn[:, t, :])
                last.then_inc(mv_done, 1)

            def normalise(kind, c):
                n = fill_no(kind, c)
                dve.wait_ge(rstd_done, n + 1)
                if not isinstance(n, int) or n > 0:
                    dve.wait_ge(xt_ps, fill_no(kind, c))
                for t in range(TPC):
                    last = nc.vector.tensor_scalar(xn[:, t, :], x[:, bass.ds(c * TPC + t, 1), :].rearrange("p o n -> p (o n)"),
                                                   mv[:, t, 0:1], rstd[:, t:t + 1], ALU.subtract, ALU.mult)
                last.then_inc(xn_done, 1)

            def fill_lo(kind, c):
                dve.wait_ge(xt_hi, fill_no(kind, c) + 1)
                for d in range(ND):
                    view = [xt[:, bass.ds(c, 1), part, d, :].rearrange("p o t -> p (o t)") for part in range(2)]
                    last = nc.vector.tensor_tensor(view[1], ps_t[:, d, :], view[0].bitcast(F32), ALU.subtract)
                last.then_inc(xt_lo, 1)

            def add_attention(c, place=T_BANKS):
                dve.wait_ge(wo_done, c + 1)
                for i in range(2):
                    xc = x[:, bass.ds(c * TPC + 2 * i, 2), :]
                    last = nc.vector.tensor_tensor(xc, xc, place[i].rearrange("p (a n) -> p a n", a=2), ALU.add)
                last.then_inc(att_added, 1)

            def at_fill_lo(c):
                dve.wait_ge(at_hi, c + 1)
                for d in range(ND):
                    last = nc.vector.tensor_tensor(xa[:, 1, d, :], ps_t[:, d, :], xa[:, 0, d, :].bitcast(F32), ALU.subtract)
                last.then_inc(at_lo, 1)

            def fill_both(ready, n, dst, hi_done, lo_done):
                dve.wait_ge(ready, n)
                for d in range(ND):
                    last = nc.vector.tensor_copy(dst(0, d), FREE_BANKS[d])
                last.then_inc(hi_done, 1)
                dve.wait_ge(hi_done, n)
                for d in range(ND):
                    last = nc.vector.tensor_tensor(dst(1, d), FREE_BANKS[d], dst(0, d).bitcast(F32), ALU.subtract)
                last.then_inc(lo_done, 1)

            def add_residual(phase, c):
                dve.wait_ge(down_done, RES[phase] + c + 1)
                for i in range(2):
                    xc = x[:, bass.ds(c * TPC + 2 * i, 2), :]
                    last = nc.vector.tensor_tensor(xc, xc, ps_down[:, i, :].rearrange("p (a n) -> p a n", a=2), ALU.add)
                last.then_inc(res_added, 1)

            def butterflies(stage_no):
                if stage_no:
                    dve.wait_ge(fly_diff, stage_no)
                    dve.wait_ge(fly_sum, stage_no)
                else:
                    dve.wait_ge(ld_w2, 16)
                a, b, s_, _ = fly_views(stage_no)
                nc.vector.tensor_tensor(s_, a, b, ALU.add).then_inc(fly_sum, 1)

            def w13_part(n):
                w, raw = ((w1, w1_raw), (w3, w3_raw))[n % 2]
                dve.wait_ge(w13_hi, n + 1)
                cols = slice((n // 2) * WP, (n // 2 + 1) * WP)
                nc.vector.tensor_tensor(w[:, 1, :, cols], raw[:, :, cols], w[:, 0, :, cols].bitcast(F32),
                                        ALU.subtract).then_inc(w13_lo, 1)

            def product(k, hc):
                dve.wait_ge(silu_done, k + 1)
                dve.wait_ge(lin_done, k + 1)
                nc.vector.tensor_tensor(u[:, hc % 2, :], u[:, hc % 2, :], ps_lin[hc % 2][:], ALU.mult
                                        ).then_inc(u_done, 1)

            def hidden_lo(k, hc):
                dve.wait_ge(uh_done, k + 1)
                nc.vector.tensor_tensor(ul[:, hc % 2, :], u[:, hc % 2, :], uh[:, hc % 2, :].bitcast(F32),
                                        ALU.subtract).then_inc(ul_done, 1)

            def w2_part(i):
                dve.wait_ge(w2_hi, i + 1)
                nc.vector.scalar_tensor_tensor(
                    w2[:, 1, 2 * i:2 * i + 2, :], ps_down[:, i % 2, :].rearrange("p (a n) -> p a n", a=2), W2_SCALE,
                    w2[:, 0, 2 * i:2 * i + 2, :].bitcast(F32), ALU.mult, ALU.subtract).then_inc(w2_lo, 1)

            dve.wait_ge(ld_x[0], 16)
            statistics("IN", 0)
            butterflies(0)
            normalise("IN", 0)
            w13_part(0)
            w13_part(1)
            butterflies(1)
            fill_lo("IN", 0)
            butterflies(2)
            for hc in range(NH):
                if hc in (0, 2, 4):
                    dve.wait_ge(ld_x[hc // 2 + 1], 16)
                    statistics("IN", hc // 2 + 1)
                product(hc, hc)
                if hc < 2:
                    w2_part(2 * hc)
                    w2_part(2 * hc + 1)
                hidden_lo(hc, hc)
                if hc < 3:
                    w13_part(2 * hc + 2)
                    w13_part(2 * hc + 3)
                if hc in (1, 3, 5):
                    normalise("IN", (hc + 1) // 2)
                if hc in (2, 4, 6):
                    fill_lo("IN", hc // 2)
            dve.wait_ge(ld_const, 16 * 7)
            nc.vector.tensor_copy(ident_b[:], ident[:]).then_inc(const_cut, 1)
            nc.vector.tensor_copy(tri_b[:], tri_f[:]).then_inc(const_cut, 1)
            nc.vector.tensor_copy(sides[:], sides_f[:]).then_inc(const_cut, 1)

            def feed_forward(layer, c, extra):
                for hc in range(NH):
                    k = (layer * NC + c) * NH + hc
                    product(k, hc)
                    hidden_lo(k, hc)
                    extra(hc)

            def tail(phase, norm, c):
                def extra(hc):
                    if hc == 0:
                        add_residual(phase, c)
                    if norm and hc == 1:
                        dve.wait_ge(res_added, RES[phase] + c + 1)
                        statistics(norm, c)
                    if norm and hc == 2:
                        normalise(norm, c)
                    if norm and hc == 3:
                        fill_lo(norm, c)
                return extra

            with dve.Fori(1, NC) as c:
                feed_forward(0, c, tail("FF", "FF", c - 1))

            def values_in(i):
                dve.wait_ge(v_ps, i + 1)
                b, j = i // 4, 2 * (i % 4)
                for tt in range(2):
                    last = nc.vector.tensor_tensor(
                        v_all[:, j + tt, b * GROUPS:(b + 1) * GROUPS, :],
                        banks[2 + i % 2][:, tt * D:(tt + 1) * D].rearrange("p (g n) -> p g n", g=GROUPS),
                        bv[:].rearrange("p (g n) -> p g n", g=GROUPS), ALU.add)
                last.then_inc(v_done, 1)

            def last_part(k):
                dve.wait_ge(qm_done, k + 1)
                nc.vector.tensor_tensor(stage[:, k % QBUF, staged(k, 2), :], r1[:, k % 2, :], stage[:, k % QBUF, staged(k, 1), :],
                                        ALU.subtract).then_inc(ql_done, 1)

            end = tail("FF", "FF", NC - 1)
            end(0)
            for k in range(4 * NC):
                if k == 4 * NC - 1:
                    values_in(2 * NC - 2)
                    values_in(2 * NC - 1)
                dve.wait_ge(qh_done, k + 1)
                if k >= 2:
                    dve.wait_ge(qm_done, k - 1)
                    dve.wait_ge(ql_done, k - 1)
                nc.vector.tensor_tensor(r1[:, k % 2, :], qf[:, k % 2, :], stage[:, k % QBUF, staged(k, 0), :], ALU.subtract
                                        ).then_inc(r1_done, 1)
                if k >= 1:
                    last_part(k - 1)
                if k < 2:
                    end(k + 1)
                if k == LAST_FILL - 1:
                    end(3)
                if k % 4 == 3 and k < 4 * NC - 1:
                    values_in(2 * (k // 4))
                    values_in(2 * (k // 4) + 1)
            last_part(4 * NC - 1)

            def ring_item(item, bank, after_count, unit, par, prev_unit):
                kind, a, h, piece = item
                dve.wait_ge(ring_full, after_count)
                src = ps_ring[bank]
                if kind == "red":
                    n, heads = red_width(a, piece), red_heads(a, piece)
                    at = (a if a < TPC else 2 * a - TPC + piece) * GH + h
                    nc.vector.reduce_max(mp[:, at:at + heads], src[:, 0:heads * n].rearrange("p (h n) -> p h n", n=n), AX.X
                                         ).then_inc(ring_free, 1)
                    if item == RED_B[-1]:
                        dve.wait_ge(ring_free, after_count)
                        two = mp[:, MA:3 * MA].rearrange("p (i c h) -> p c h i", c=2, h=GH)
                        nc.vector.tensor_tensor(mb[:], two[:, 0], two[:, 1], ALU.max).then_inc(mb_done, 1)
                        dve.wait_ge(mb_done, unit + 1)
                        nc.vector.scalar_tensor_tensor(mneg[:, par, :, TPC:KT], mb[:], -1.0, neg_floor[:],
                                                       ALU.mult, ALU.min).then_inc(mneg_done, 1)
                        dve.wait_ge(mneg_done, unit + 1)
                        cut_maxima(nc.vector, dve.wait_ge, unit, par, 1)
                elif kind == "mt":
                    if not isinstance(unit, int) or unit > 0:
                        dve.wait_ge(mrow_in[a], unit * 16)
                    nc.vector.tensor_copy(mt[:, a, :], src[0:PARTS * MT, 0:P // 2].bitcast(BF16)).then_inc(ring_free, 1)
                else:
                    oc = prev_unit * 2 + a
                    cols = slice(a * TPC, (a + 1) * TPC)
                    four = src[:].rearrange("p (t h n) -> p t h n", t=TPC, h=GH)
                    dve.wait_ge(em_done, prev_unit + 1)
                    dve.wait_ge(o_done, oc + 1)
                    nc.vector.tensor_tensor(dsum[:], four[:, :, :, HD], ecnt[:, :, cols].rearrange("p h t -> p t h"),
                                            ALU.add).then_inc(dsum_done, 1)
                    nc.vector.tensor_tensor(num[:], four[:, :, :, 0:HD], em[:, cols], ALU.add
                                            ).then_inc(ring_free, 1)
                    dve.wait_ge(dsum_done, oc + 1)
                    nc.vector.reciprocal(rcp[:], dsum[:]).then_inc(rcp_done, 1)

            for n, item in enumerate(FIRST_ITEMS):
                ring_item(item, (n + 2) % RING, n + 1, 0, 0, None)

            def body(unit, par, last):
                ring0 = NFIRST + unit * NBODY
                items = BODY_ITEMS if not last else LAST_ITEMS
                if last:
                    fill_both(at_ps, 1, lambda part, d: xa[:, part, d, :], at_hi, at_lo)
                    dve.wait_ge(bo_added, 1)
                    add_attention(0, FREE_BANKS)
                    dve.wait_ge(att_added, 1)
                    statistics("OUT", 0)
                for n, item in enumerate(items):
                    ring_item(item, n % RING if not last else n, ring0 + n + 1, unit + 1, 1 - par, unit)
                    if last and n == 0:
                        normalise("OUT", 0)
                        fill_both(xt_ps, fill_no("OUT", 0) + 1, lambda part, d: xt[:, 0, part, d, :], xt_hi, xt_lo)

            with dve.Fori(0, UNITS // 2 - 1) as it:
                body(it * 2, 0, False)
                body(it * 2 + 1, 1, False)
            body(UNITS - 2, 0, False)
            body(UNITS - 1, 1, True)

            dve.wait_ge(o_done, UNITS * 2 + 1)

            def following(before, c):
                def extra(hc):
                    if hc == 0:
                        if before is not None:
                            add_residual("FF2", before)
                        if c is not None:
                            at_fill_lo(c)
                    if c is not None and hc == 3:
                        add_attention(c)
                        dve.wait_ge(att_added, c + 1)
                        statistics("OUT", c)
                    if c is not None and hc == 4:
                        normalise("OUT", c)
                    if c is not None and hc == 5:
                        fill_lo("OUT", c)
                return extra

            feed_forward(1, 0, following(None, 1))
            with dve.Fori(1, NC - 1) as c:
                feed_forward(1, c, following(c - 1, c + 1))
            feed_forward(1, NC - 1, following(NC - 2, None))
            add_residual("FF2", NC - 1)

        @block.gpsimd
        def _(pool):
            nc.gpsimd.memset(neg_half[:], -0.5).then_inc(pool_const, 1)

            def inverse_deviation(kind, c):
                n = fill_no(kind, c)
                loop_wait(pool, mv_done, n + 1)
                if not isinstance(n, int) or n > 0:
                    loop_wait(pool, xn_done, n)
                nc.gpsimd.tensor_scalar_add(ve[:], mv[:, :, 1], EPS).then_inc(ve_done, 1)
                loop_wait(pool, ve_done, n + 1)
                nc.gpsimd.tensor_tensor(rstd[:], ve[:], neg_half[:], ALU.pow).then_inc(rstd_done, 1)

            pool.wait_ge(pool_const, 1)
            inverse_deviation("IN", 0)
            for stage_no in range(3):
                if stage_no:
                    pool.wait_ge(fly_sum, stage_no)
                    pool.wait_ge(fly_diff, stage_no)
                else:
                    pool.wait_ge(ld_w2, 16)
                a, b, _, d_ = fly_views(stage_no)
                nc.gpsimd.tensor_tensor(d_, a, b, ALU.subtract).then_inc(fly_diff, 1)
            for c in range(1, NC):
                inverse_deviation("IN", c)
            for n, (w, raw, loaded) in enumerate(((wqkv, wqkv_raw, ld_wqkv), (wo, wo_raw, ld_wo))):
                pool.wait_ge(loaded, 16)
                nc.gpsimd.tensor_copy(w[:, 0], raw[:]).then_inc(wsplit_hi, 1)
                pool.wait_ge(wsplit_hi, n + 1)
                nc.gpsimd.tensor_tensor(w[:, 1], raw[:], w[:, 0].bitcast(F32), ALU.subtract).then_inc(wsplit_lo, 1)
                pool.wait_ge(wsplit_lo, n + 1)
            with pool.Fori(1, NC) as c:
                inverse_deviation("FF", c - 1)
            def take_output(c):
                pool.wait_ge(at_ps, c)
                b, j0 = c // 2, c % 2 * TPC
                nc.gpsimd.tensor_copy(o_now[:].rearrange("p j (g n) -> p j g n", g=GROUPS),
                                      o_tok[:, j0:j0 + TPC, b * GROUPS:(b + 1) * GROUPS, :]).then_inc(o_taken, 1)

            pool.wait_ge(w13_lo, 2 * WSPLIT)
            pool.wait_ge(w2_lo, NH // 2)
            pool.wait_ge(rstd_done, 2 * NC - 1)
            nc.gpsimd.memset(ks[SROWS:MROWS], 1.0).then_inc(stack_ones, 1)
            pool.wait_ge(stack_ones, 1)
            inverse_deviation("FF", NC - 1)
            pool.wait_ge(ld_const, 16 * 7)
            for c in range(NC):
                pool.wait_ge(xn_done, fill_no("FF", c) + 1)
                last = nc.gpsimd.tensor_tensor(chunk_of(x, c), chunk_of(x, c), bo[:].unsqueeze(1).broadcast_to([P, TPC, D]),
                                               ALU.add)
            last.then_inc(bo_added, 1)

            pool.wait_ge(down_done, NC)
            nc.gpsimd.memset(vg[:], 1.0).then_inc(vg_ones, 1)
            nc.gpsimd.memset(num[:], 0.0).then_inc(o_done, 1)
            pool.wait_ge(v_done, 2 * NC)
            pool.wait_ge(vg_ones, 1)

            def take_values(unit, par):
                if not isinstance(unit, int) or unit >= 1:
                    loop_wait(pool, pv_done, (unit - 1) * NSTEP + 1)
                nc.gpsimd.tensor_copy(vg[:, par, :, :, 0:HD],
                                      v_all[:, :, bass.ds(unit, 1)].rearrange("p j o (h n) -> p (j o) h n", h=GH)
                                      ).then_inc(vg_done, 1)

            def front_maxima(unit, par):
                if isinstance(unit, int) and unit == 0:
                    pool.wait_ge(ring_free, NA)
                else:
                    loop_wait(pool, ring_free, ring_count(unit - 1, RED_A[-1]))
                nc.gpsimd.tensor_scalar(mneg[:, par, :, 0:TPC], mp[:, 0:MA].rearrange("p (i h) -> p h i", h=GH),
                                        MASKED / SCALE, -1.0, ALU.max, ALU.mult).then_inc(front_done, 1)
                loop_wait(pool, front_done, unit + 1)
                cut_maxima(nc.gpsimd, lambda *count: loop_wait(pool, *count), unit, par, 0)

            def mask(step, s):
                loop_wait(pool, p_done, step * 2 + 2)
                tile = probs[:, s % RING, :, 0:P]
                nc.gpsimd.affine_select(out=tile, in_=tile, compare_op=ALU.is_ge, fill=0.0, base=0,
                                        pattern=[[0, GH], [1, P]], channel_multiplier=-1).then_inc(p_masked, 1)

            def masked_share(unit, par):
                nc.gpsimd.tensor_scalar(ea[:], mneg[:, par], SCALE, -MASKED, ALU.mult, ALU.min).then_inc(ea_step, 1)
                loop_wait(pool, ea_step, unit * 2 + 1)
                nc.gpsimd.tensor_scalar_add(ea[:], ea[:], MASKED).then_inc(ea_done, 1)
                loop_wait(pool, et_done, unit + 1)
                nc.gpsimd.tensor_tensor(ecnt[:], et[:, par], count[:].unsqueeze(1).broadcast_to([P, GH, KT]),
                                        ALU.mult).then_inc(ea_step, 1)
                loop_wait(pool, ea_step, unit * 2 + 2)
                nc.gpsimd.tensor_tensor(
                    em[:], suffix[:, :, bass.ds(unit, 1)].rearrange("p j o (h n) -> p (j o) h n", h=GH),
                    et[:, par].rearrange("p h t -> p t h").unsqueeze(3).broadcast_to([P, KT, GH, HD]),
                    ALU.mult).then_inc(em_done, 1)

            def scale_o(unit, c):
                oc = unit * 2 + c
                loop_wait(pool, rcp_done, oc + 1)
                nc.gpsimd.tensor_tensor(
                    o_tok[:, c * TPC:(c + 1) * TPC, bass.ds(unit, 1)].rearrange("p j o (h n) -> p (j o) h n", h=GH),
                    num[:], rcp[:].unsqueeze(3).broadcast_to([P, TPC, GH, HD]), ALU.mult).then_inc(o_done, 1)

            def value_lo(n):
                pool.wait_ge(vs_hi, n + 1)
                nc.gpsimd.tensor_tensor(split_values(n, 1), v_all[:, KT - 1 - n].rearrange("p u n -> p (u n)"),
                                        split_values(n, 0).bitcast(F32), ALU.subtract).then_inc(vs_lo, 1)

            for n in range(KT):
                if n == LO_FIRST:
                    front_maxima(0, 0)
                value_lo(n)
            take_values(0, 0)
            for s in range(AHEAD):
                if s in DIAG:
                    mask(s, s)
            pool.wait_ge(suf_done, KT)

            def body(unit, par, last):
                for t in range(NSTEP if not last else NSTEP - AHEAD):
                    s = (AHEAD + t) % NSTEP
                    if s in DIAG:
                        mask(unit * NSTEP + (AHEAD + t), s)
                    if t == 0:
                        masked_share(unit, par)
                        if not last:
                            take_values(unit + 1, 1 - par)
                    if last and t == AT_SLOT + 1:
                        pool.wait_ge(em_done, UNITS)
                        take_output(1)
                    if last and t == WO_SLOT + 1:
                        inverse_deviation("OUT", 0)
                    if t == 4:
                        if not last:
                            front_maxima(unit + 1, 1 - par)
                        scale_o(unit, 0)
                scale_o(unit, 1)

            with pool.Fori(0, UNITS // 2 - 1) as it:
                body(it * 2, 0, False)
                body(it * 2 + 1, 1, False)
            body(UNITS - 2, 0, False)
            body(UNITS - 1, 1, True)

            for c in range(1, NC):
                if c == 2:
                    pool.wait_ge(o_done, UNITS * 2 + 1)
                if c > 1:
                    take_output(c)
                inverse_deviation("OUT", c)


def constants():
    p = np.arange(P)
    bits = p[:, None] & p[None, :]
    odd = np.zeros((P, P), np.int64)
    for b in range(P.bit_length()):
        odd ^= (bits >> b) & 1
    floor = np.full((P, GH, KT // 2), -MASKED / SCALE, np.float32)
    floor[P - 1, :, KT // 2 - 1] = 3e38
    return {
        "had": (1.0 - 2.0 * odd).astype(np.float32),
        "ident": np.eye(P, dtype=np.float32),
        "tri": np.where(p[None, :] > p[:, None], NEG_BIG, 0.0).astype(np.float32),
        "after": np.stack([p[:, None] > p[None, :], p[:, None] <= p[None, :]], axis=1).astype(np.float32),
        "count": (SEQ - 1 - (p[:, None] + P * np.arange(KT)[None, :])).astype(np.float32),
        "floor": floor,
    }


def kernel(L0_attn_x, L0_attn_Wqkv, L0_attn_bqkv, L0_attn_Wo, L0_attn_bo, L0_ffn_W1, L0_ffn_W2, L0_ffn_W3):
    import concourse.bacc as bacc
    from concourse.bass_utils import run_bass_kernel_spmd

    bqkv = np.asarray(L0_attn_bqkv)
    arrays = {
        "x": np.ascontiguousarray(np.asarray(L0_attn_x).reshape(TOKENS, D)),
        "w1t": np.ascontiguousarray(np.asarray(L0_ffn_W1).T),
        "w3t": np.ascontiguousarray(np.asarray(L0_ffn_W3).T),
        "w2t": np.ascontiguousarray(np.asarray(L0_ffn_W2).T),
        "wqkv": np.ascontiguousarray(np.asarray(L0_attn_Wqkv)),
        "wo": np.ascontiguousarray(np.asarray(L0_attn_Wo)),
        "bqk": np.ascontiguousarray(bqkv[:2 * D].reshape(4, P).T),
        "bv": np.ascontiguousarray(bqkv[2 * D:].reshape(1, D)),
        "bo": np.ascontiguousarray(np.asarray(L0_attn_bo).reshape(1, D)),
        **constants(),
    }
    nc = bacc.Bacc("TRN2", target_bir_lowering=False, num_devices=1)
    args = [nc.dram_tensor("in_" + n, a.shape, mybir.dt.from_np(a.dtype), kind="ExternalInput").ap() for n, a in arrays.items()]
    out = nc.dram_tensor("out_tokens", (TOKENS, D), F32, kind="ExternalOutput").ap()
    macaron(nc, *args, out)
    r = run_bass_kernel_spmd(nc, [{"in_" + n: a for n, a in arrays.items()}], core_ids=[0])
    return r.results[0]["out_tokens"].reshape(BATCH, SEQ, D)
```
